# Optimizing a Trainium2 kernel written in Bass

```python
import numpy as np
import jax
import jax.numpy as jnp

def _softmax(x, axis=-1):
    return jax.nn.softmax(x, axis=axis)

def _gelu(x):
    return jax.nn.gelu(x, approximate=True)

def _silu(x):
    return jax.nn.silu(x)

def _sigmoid(x):
    return jax.nn.sigmoid(x)

def _layernorm(x, axis=-1, eps=1e-05):
    m = jnp.mean(x, axis=axis, keepdims=True)
    v = jnp.var(x, axis=axis, keepdims=True)
    return (x - m) / jnp.sqrt(v + eps)

def _scatter_add(tgt, idx, src, axis=0):
    return tgt.at[idx].add(src)

def _segment_sum(src, seg, n):
    return jax.ops.segment_sum(src, seg, n)
kernel_name = 'mk_adj_resnorm_d2_adj_r2_614c04'

def setup_inputs(seed: int=0):
    np.random.seed(seed)
    _w = jnp.asarray

    def _rec_inputs():
        import jax
        import jax.numpy as jnp
        _gk = jax.random.key(seed)
        x = 7.22e-05 + 1 * jax.random.normal(jax.random.fold_in(_gk, 1), (8, 1024, 128), jnp.float32)
        _a = jax.random.bernoulli(jax.random.fold_in(_gk, 2), 0.00195312, (1024, 1024))
        _a = jnp.logical_or(_a, jnp.swapaxes(_a, -1, -2))
        _a = jnp.logical_or(_a, jnp.eye(1024, dtype=bool))
        _af = _a.astype(jnp.float32)
        _af = _af * jax.random.uniform(jax.random.fold_in(_gk, 3), (1024, 1024), jnp.float32, 0.05, 0.000976562)
        adj = _af
        return (x, adj)
    x, adj = _rec_inputs()

    def _L0_gnn_setup():
        import jax, jax.numpy as jnp
        import numpy as np
        B, N, F_IN, F_OUT, ORDERS = (32, 1024, 128, 128, 2)
        NUM_MATRICES = 2 * ORDERS + 1

        def _cheb_hops(x0, A, orders):
            hops = []
            x1 = jnp.einsum('bnf,nw->bwf', x0, A)
            hops.append(x1)
            xk_1, xk_2 = (x1, x0)
            for _ in range(2, orders + 1):
                x2 = 2.0 * jnp.einsum('bnf,nw->bwf', xk_1, A) - xk_2
                hops.append(x2)
                xk_1, xk_2 = (x2, xk_1)
            return hops
        key = jax.random.key(seed)
        k1, k2, k3, k4, k5 = jax.random.split(key, 5)
        X = jax.random.normal(k1, (B, N, F_IN), dtype=jnp.float32)
        A1 = jax.random.uniform(k2, (N, N), dtype=jnp.float32) * (2.0 / N)
        A2 = jax.random.uniform(k3, (N, N), dtype=jnp.float32) * (2.0 / N)
        stdv = 1.0 / np.sqrt(F_OUT)
        Theta1 = jax.random.uniform(k4, (F_IN * NUM_MATRICES, F_OUT), dtype=jnp.float32, minval=-stdv, maxval=stdv)
        bias = jax.random.uniform(k5, (F_OUT,), dtype=jnp.float32, minval=-stdv, maxval=stdv)
        return {'X': X, 'A1': A1, 'A2': A2, 'Theta1': Theta1, 'bias': bias}
    _L0_gnn_all = _L0_gnn_setup()
    _L0_gnn_in = {k: v for k, v in _L0_gnn_all.items() if k in ('Theta1', 'bias')}
    del _L0_gnn_all

    def _L1_gnn_setup():
        import jax, jax.numpy as jnp
        import numpy as np
        _NEG_INF = -1000000000.0
        ALPHA = 0.2
        key = jax.random.key(seed)
        k0, k1, k2, k3, k4 = jax.random.split(key, 5)
        B, N, F_IN, F_OUT = (8, 1024, 128, 128)
        x = jax.random.normal(k0, (B, N, F_IN), dtype=jnp.float32)
        adj = (jax.random.uniform(k1, (N, N)) < 0.02).astype(jnp.float32)
        W = jax.random.normal(k2, (F_IN, F_OUT), dtype=jnp.float32) * (1.0 / np.sqrt(F_IN))
        bound = float(np.sqrt(6.0 / (F_OUT + 1)))
        a_src = jax.random.uniform(k3, (F_OUT, 1), minval=-bound, maxval=bound, dtype=jnp.float32)
        a_dst = jax.random.uniform(k4, (F_OUT, 1), minval=-bound, maxval=bound, dtype=jnp.float32)
        return {'x': x, 'adj': adj, 'W': W, 'a_src': a_src, 'a_dst': a_dst}
    _L1_gnn_all = _L1_gnn_setup()
    _L1_gnn_in = {k: v for k, v in _L1_gnn_all.items() if k in ('W', 'a_src', 'a_dst')}
    del _L1_gnn_all
    return {'x': x, 'adj': adj, 'L0_gnn_Theta1': _L0_gnn_in['Theta1'], 'L0_gnn_bias': _L0_gnn_in['bias'], 'L1_gnn_W': _L1_gnn_in['W'], 'L1_gnn_a_src': _L1_gnn_in['a_src'], 'L1_gnn_a_dst': _L1_gnn_in['a_dst']}

def reference(x, adj, L0_gnn_Theta1, L0_gnn_bias, L1_gnn_W, L1_gnn_a_src, L1_gnn_a_dst):
    import jax
    import jax.numpy as jnp

    def _L0_gnn_ref(X, A1, A2, Theta1, bias):
        import jax, jax.numpy as jnp
        import numpy as np
        B, N, F_IN, F_OUT, ORDERS = (32, 1024, 128, 128, 2)
        NUM_MATRICES = 2 * ORDERS + 1

        def _cheb_hops(x0, A, orders):
            hops = []
            x1 = jnp.einsum('bnf,nw->bwf', x0, A)
            hops.append(x1)
            xk_1, xk_2 = (x1, x0)
            for _ in range(2, orders + 1):
                x2 = 2.0 * jnp.einsum('bnf,nw->bwf', xk_1, A) - xk_2
                hops.append(x2)
                xk_1, xk_2 = (x2, xk_1)
            return hops
        xs = [X] + _cheb_hops(X, A1, ORDERS) + _cheb_hops(X, A2, ORDERS)
        x = jnp.stack(xs, axis=2)
        b, n = (X.shape[0], X.shape[1])
        x = x.reshape(b, n, -1)
        out = jax.nn.relu(x @ Theta1 + bias)
        return out

    def _L1_gnn_ref(x, adj, W, a_src, a_dst):
        import jax, jax.numpy as jnp
        import numpy as np
        _NEG_INF = -1000000000.0
        ALPHA = 0.2
        h = jnp.einsum('bnf,fo->bno', x, W)
        N = h.shape[1]
        e_src = (h @ a_src)[..., 0]
        e_dst = (h @ a_dst)[..., 0]
        e = jax.nn.leaky_relu(e_src[:, :, None] + e_dst[:, None, :], negative_slope=ALPHA)
        adj_loops = jnp.clip(adj + jnp.eye(N, dtype=adj.dtype), 0.0, None)
        e = jnp.where(adj_loops[None, :, :] == 0, _NEG_INF, e)
        attn = jax.nn.softmax(e, axis=-1)
        attn = jnp.nan_to_num(attn, nan=0.0, posinf=0.0, neginf=0.0)
        h_prime = jnp.einsum('bij,bjo->bio', attn, h)
        return jax.nn.elu(h_prime)
    x = _layernorm(x + _L0_gnn_ref(x, adj, adj, L0_gnn_Theta1, L0_gnn_bias), axis=-1)
    x = _layernorm(x + _L1_gnn_ref(x, adj, L1_gnn_W, L1_gnn_a_src, L1_gnn_a_dst), axis=-1)
    return x

_drawn_inputs = setup_inputs


def setup_inputs(seed=0):
    import zlib

    import numpy as np

    out = dict(_drawn_inputs(seed))
    spreads = {}
    factors = {}
    for name, (base, spread) in spreads.items():
        noise = np.random.default_rng([zlib.crc32(name.encode()), seed]).standard_normal(out[name].shape)
        drawn = base * np.exp(spread * noise) if base else spread * noise
        out[name] = jnp.asarray(drawn.astype(out[name].dtype))
    for name, factor in factors.items():
        out[name] = (out[name] * factor).astype(out[name].dtype)
    return out
```

```python
from contextlib import ExitStack

import concourse.bass as bass
from concourse import mybir

F32, F32R, BF16, U8 = mybir.dt.float32, mybir.dt.float32r, mybir.dt.bfloat16, mybir.dt.uint8
ALU = mybir.AluOpType
ACT = mybir.ActivationFunctionType

P = 128
B, N, F = 8, 1024, 128
K = N // P
PAIR = 2
GROUPS = B // PAIR
SLOTS = 2 * K
STEPS = PAIR * K
RING = 8
HB, MB = 2, 3
BANK = 512
HW = F + 3
PVW = F + 1
PV_PER_BANK = BANK // PVW
PV_BANKS = -(-K // PV_PER_BANK)
ALPHA, EPS, MASKED = 0.2, 1e-5, -1e30
XT_TILE, D_TILE, JUNK_TILE = 3, 5, 7

MAXES = {0: (0, range(0, 2)), 1: (0, range(2, 4)), 2: (0, range(4, 6)), 3: (0, range(6, 8)),
         4: (1, range(0, 4)), 5: (1, range(4, 8))}
STEPS_IN = {5: [0], 6: [1, 2], 7: [3, 4], 8: [5, 6], 9: [7], 10: [8], 11: [9, 10],
            12: [11, 12], 13: [13], 14: [14], 15: [15]}
EPI_SLOT = 10


class Signal:

    def __init__(self, sem, per, first, unit=1):
        self.sem, self.per, self.first, self.unit = sem, per, first, unit

    def level(self, t, i):
        return (t - self.first) * (self.per * self.unit) + (i + 1) * self.unit


def wait(eng, signal, t, i, up=None):
    level = signal.level(t, i)
    if up is not None:
        if not isinstance(level, int):
            register = eng.alloc_register()
            eng.reg_mov(register, level)
            level = register
        eng.wait_ge(up, 1)
    eng.wait_ge(signal.sem, level)
    if up is not None and not isinstance(level, int):
        eng.free_register(level)


def chebyshev_then_attention(nc, x, xt, adj, adjt, theta, bias, w, wt, a_src, a_dst, ident_in, out):
    with ExitStack() as ctx:
        def sb(name, shape, dt=F32):
            return ctx.enter_context(nc.sbuf_tensor(name, shape, dt))

        def sem(name):
            return ctx.enter_context(nc.semaphore(name))

        a_hi = sb("a_hi", [P, K, N], F32R)
        a_lo = sb("a_lo", [P, K, N], F32R)
        neg = sb("neg", [P, K, N], BF16)
        mask_t = sb("mask_t", [P, K, N], U8)
        y_hi = sb("y_hi", [P, K, PAIR * F], F32R)
        y_lo = sb("y_lo", [P, K, PAIR * F], F32R)
        z_hi = sb("z_hi", [P, K, PAIR * F], F32R)
        z_lo = sb("z_lo", [P, K, PAIR * F], F32R)
        xt_sb = sb("xt_sb", [P, K, PAIR, P])
        xn = sb("xn", [P, PAIR, K, F])
        xres = sb("xres", [P, PAIR, K, F])
        haug = sb("haug", [P, PAIR, K, HW])
        rows_ab = sb("rows_ab", [P, PAIR, 2, N])
        ring = sb("ring", [P, RING, N])
        ident = sb("ident", [P, P])
        t24 = sb("t24", [P, F])
        t13 = sb("t13", [P, F])
        t0 = sb("t0", [P, F])
        w_aug = sb("w_aug", [P, F + 2])
        ones = sb("ones", [P, P], F32R)
        bias_r = sb("bias_r", [P, PAIR * F], F32R)
        minus_half = sb("minus_half", [P, 2 * K])
        stats1 = sb("stats1", [P, PAIR, 6])
        mv1 = sb("mv1", [P, K, PAIR, 2])
        rstd1 = sb("rstd1", [P, K, PAIR])
        stats2 = sb("stats2", [P, K, 6])
        mv2 = sb("mv2", [P, K, 2])
        rstd2 = sb("rstd2", [P, K])
        d_col = sb("d_col", [P, PAIR, K])
        d02 = sb("d02", [P, PAIR, K])
        dmax = sb("dmax", [P, K])
        logit = sb("logit", [P, K])
        m_col = sb("m_col", [P, K])
        ab_col = sb("ab_col", [P, PAIR, 2, K])
        rsum = sb("rsum", [P, PAIR, K])
        hop_ps = ctx.enter_context(nc.psum_tensor("hop_ps", [P, HB, BANK], F32))
        misc_ps = ctx.enter_context(nc.psum_tensor("misc_ps", [P, MB, BANK], F32))
        pv_ps = ctx.enter_context(nc.psum_tensor("pv_ps", [P, PV_BANKS, BANK], F32))
        d_row = nc.dram_tensor("d_row", [PAIR, P, K], F32, kind="Internal").ap()
        ab_row = nc.dram_tensor("ab_row", [PAIR, P, 2, K], F32, kind="Internal").ap()

        consts_in, theta_in = sem("consts_in"), sem("theta_in")
        a_in = [sem(f"a_in{k}") for k in range(K)]
        at_in = [sem(f"at_in{k}") for k in range(K)]
        a_hi_done, a_lo_done, neg_done, mask_done = sem("a_hi_done"), sem("a_lo_done"), sem("neg_done"), sem("mask_done")
        theta_done, wa_mm, w_done, half_done, bias_done, dve_setup = (
            sem("theta_done"), sem("wa_mm"), sem("w_done"), sem("half_done"), sem("bias_done"), sem("dve_setup"))
        xt_in = [Signal(sem(f"xt_in{c}"), 1, 0, 16) for c in range(K)]
        x_in = Signal(sem("x_in"), 1, 0, 16)
        y_mm, y_hi_done, y_lo_done = (Signal(sem(s), K, 0) for s in ("y_mm", "y_hi_done", "y_lo_done"))
        hop_mm = Signal(sem("hop_mm"), SLOTS, 0)
        z_hi_done, z_lo_done = (Signal(sem(s), K, 0) for s in ("z_hi_done", "z_lo_done"))
        x1_done, bn1_done, mv1_done, eps1_done, rstd1_done, xn_done = (
            Signal(sem(s), K, 0) for s in ("x1_done", "bn1_done", "mv1_done", "eps1_done", "rstd1_done", "xn_done"))
        tr_mm, xt_ev, h_mm, h_ev = (Signal(sem(s), K, 1) for s in ("tr_mm", "xt_ev", "h_mm", "h_ev"))
        xres_in = Signal(sem("xres_in"), PAIR, 1, 16)
        d_ready, ab_ready = (Signal(sem(s), PAIR, 1) for s in ("d_ready", "ab_ready"))
        d_out, ab_out = (Signal(sem(s), PAIR, 1, 16) for s in ("d_out", "ab_out"))
        d_in = [Signal(sem(f"d_in{b}"), 1, 1, 16) for b in range(PAIR)]
        ab_in = [Signal(sem(f"ab_in{b}"), 1, 1, 16) for b in range(PAIR)]
        max_done, logit_done, m_done = Signal(sem("max_done"), STEPS, 1), Signal(sem("logit_done"), PAIR, 1), Signal(sem("m_done"), PAIR, 1)
        t2_done, z_done, exp_done, p_done, pv_mm = (
            Signal(sem(s), STEPS, 1) for s in ("t2_done", "z_done", "exp_done", "p_done", "pv_mm"))
        rsum_done, elu_done, w_sum, y_done, bn2_done, mv2_done, eps2_done, rstd2_done, out_done = (
            Signal(sem(s), PAIR, 1) for s in
            ("rsum_done", "elu_done", "w_sum", "y_done", "bn2_done", "mv2_done", "eps2_done", "rstd2_done", "out_done"))
        out_stored = Signal(sem("out_stored"), PAIR, 1, 16)

        def passes(eng, one_pass):
            one_pass(0, True, False)
            with eng.Fori(1, GROUPS) as t:
                one_pass(t, True, True)
            one_pass(GROUPS, False, True)

        def misc_free(eng, t, pos, layer0_only):
            prev = pos - MB
            if prev < 0:
                wait(eng, y_lo_done, t - 1, prev + K)
            elif prev < K:
                wait(eng, xt_ev, t, prev)
            elif prev < 2 * K:
                if not layer0_only:
                    wait(eng, h_ev, t, prev - K)
            else:
                wait(eng, y_lo_done, t, prev - 2 * K)

        block = ctx.enter_context(nc.Block())

        @block.sync
        def _(sp):
            for dst, src in ((ident[:], ident_in), (w_aug[:, 0:F], w)):
                sp.dma_start(dst, src).then_inc(consts_in, 16)
            sp.dma_start(xres[:, 1, 0, :], wt).then_inc(consts_in, 16)
            sp.dma_start(xres[:, 1, 1, 0:1], a_src).then_inc(consts_in, 16)
            sp.dma_start(xres[:, 1, 1, 1:2], a_dst).then_inc(consts_in, 16)
            sp.dma_start(xres[0:1, 1, 2, :], bias).then_inc(consts_in, 16)
            sp.dma_start(xres[1:2, 1, 2, :], bias).then_inc(consts_in, 16)
            for k in range(1, K, 2):
                sp.dma_start(ring[:, k, :], adj[:, k, :]).then_inc(a_in[k], 16)
            sp.dma_start(xn[:], x[0]).then_inc(x_in.sem, 16)
            for k in range(K):
                sp.wait_ge(a_hi_done, k + 1)
                sp.wait_ge(a_lo_done, k + 1)
                sp.wait_ge(neg_done, k + 1)
                sp.dma_start(ring[:, k, :], adjt[:, k, :]).then_inc(at_in[k], 16)

            def one_pass(t, layer0, layer1):
                if not layer1:
                    return
                wait(sp, xn_done, t - 1, K - 1)
                for b in range(PAIR):
                    sp.dma_start(xres[:, b], xn[:, b]).then_inc(xres_in.sem, 16)
                if layer0:
                    wait(sp, xres_in, t, PAIR - 1, theta_done)
                    wait(sp, tr_mm, t, K - 1)
                    sp.dma_start(xn[:], x[t]).then_inc(x_in.sem, 16)
                for b in range(PAIR):
                    wait(sp, d_ready, t, b)
                    sp.dma_start(d_row[b], d_col[:, b, :]).then_inc(d_out.sem, 16)
                    wait(sp, d_out, t, b)
                    sp.dma_start(ring[:, D_TILE + b, :],
                                 d_row[b].rearrange("(o p) k -> o (p k)", o=1).broadcast_to([P, N])).then_inc(d_in[b].sem, 16)
                for b in range(PAIR):
                    wait(sp, ab_ready, t, b)
                    sp.dma_start(ab_row[b], ab_col[:, b]).then_inc(ab_out.sem, 16)
                    wait(sp, ab_out, t, b)
                    sp.dma_start(rows_ab[:, b].rearrange("p a n -> p (a n)"),
                                 ab_row[b].rearrange("(o p) a k -> o (p a k)", o=1).broadcast_to([P, 2 * N])
                                 ).then_inc(ab_in[b].sem, 16)
                wait(sp, out_stored, t, PAIR - 1, theta_done)

            passes(sp, one_pass)

        @block.gpsimd
        def _(pool):
            nc.gpsimd.memset(minus_half[:], -0.5).then_inc(half_done, 1)
            pool.wait_ge(half_done, 1)

            def rstd1_of(t, c):
                wait(pool, mv1_done, t, c, half_done)
                nc.gpsimd.tensor_scalar(rstd1[:, c, :], mv1[:, c, :, 1], EPS, 1.0, ALU.add, ALU.mult).then_inc(eps1_done.sem, 1)
                wait(pool, eps1_done, t, c)
                nc.gpsimd.tensor_tensor(rstd1[:, c, :], rstd1[:, c, :], minus_half[:, 0:PAIR], ALU.pow).then_inc(rstd1_done.sem, 1)

            def rstd2_of(t, b):
                wait(pool, mv2_done, t, b, half_done)
                nc.gpsimd.tensor_scalar(rstd2[:], mv2[:, :, 1], EPS, 1.0, ALU.add, ALU.mult).then_inc(eps2_done.sem, 1)
                wait(pool, eps2_done, t, b)
                nc.gpsimd.tensor_tensor(rstd2[:], rstd2[:], minus_half[:, 0:K], ALU.pow).then_inc(rstd2_done.sem, 1)

            def store(t, b):
                wait(pool, out_done, t, b, half_done)
                pool.dma_start(out[t - 1][:, b], xres[:, b]).then_inc(out_stored.sem, 16)

            def one_pass(t, layer0, layer1):
                for slot in range(SLOTS):
                    if layer0 and slot >= K:
                        rstd1_of(t, slot - K)
                    if layer1 and slot == EPI_SLOT:
                        rstd2_of(t, 0)
                    if layer1 and slot == EPI_SLOT + 1:
                        store(t, 0)
                if layer1:
                    rstd2_of(t, 1)
                    store(t, 1)

            passes(pool, one_pass)

        @block.scalar
        def _(act):
            act.dma_start(xres[:, 0, 0:5, :], theta).then_inc(theta_in, 16)
            for c in range(K):
                act.dma_start(xt_sb[:, c], xt[0][:, c]).then_inc(xt_in[c].sem, 16)
            for k in range(0, K, 2):
                act.dma_start(ring[:, k, :], adj[:, k, :]).then_inc(a_in[k], 16)
            act.wait_ge(wa_mm, 1)
            nc.scalar.copy(w_aug[:, F:F + 2], misc_ps[:, 0, 0:2]).then_inc(w_done, 1)

            for k in range(K):
                act.wait_ge(a_in[k], 16)
                nc.scalar.copy(a_hi[:, k, :], ring[:, k, :]).then_inc(a_hi_done, 1)

            def copy_y_hi(t, c):
                wait(act, y_mm, t, c)
                if not (isinstance(t, int) and t == 0):
                    wait(act, hop_mm, t - 1, K - 1)
                nc.scalar.copy(y_hi[:, c, :], misc_ps[:, (2 * K + c) % MB, 0:PAIR * F]).then_inc(y_hi_done.sem, 1)

            def copy_z_hi(t, c):
                wait(act, hop_mm, t, c)
                if not (isinstance(t, int) and t == 0):
                    wait(act, hop_mm, t - 1, SLOTS - 1)
                nc.scalar.copy(z_hi[:, c, :], hop_ps[:, c % HB, 0:PAIR * F]).then_inc(z_hi_done.sem, 1)

            def second_branch(t, s):
                b, k = divmod(s, K)
                if k == 0:
                    wait(act, ab_in[b], t, 0)
                if s == 0:
                    wait(act, max_done, t, STEPS - 1)
                if s >= RING:
                    wait(act, pv_mm, t, s - RING)
                nc.scalar.activation(ring[:, s % RING, :].rearrange("p (k q) -> p k q", k=K),
                                     rows_ab[:, b].rearrange("p a n -> p (a n)").rearrange("p (q a k) -> p a k q", a=2, k=K)[:, 1],
                                     ACT.Identity, bias=d02[:, b, k:k + 1], scale=1.0).then_inc(t2_done.sem, 1)

            def exp(t, s):
                wait(act, z_done, t, s)
                nc.scalar.activation(ring[:, s % RING, :], ring[:, s % RING, :], ACT.Exp).then_inc(exp_done.sem, 1)

            def elu_parts(t, b):
                wait(act, rsum_done, t, b)
                flat = rows_ab[:, b]
                for i in range(K):
                    src = pv_ps[:, i // PV_PER_BANK, (i % PV_PER_BANK) * PVW + 1:(i % PV_PER_BANK + 1) * PVW]
                    nc.scalar.activation(flat[:, 0, i * F:(i + 1) * F], src, ACT.Relu, scale=rsum[:, b, i:i + 1])
                    last = nc.scalar.activation(flat[:, 1, i * F:(i + 1) * F], src, ACT.Exp, scale=rsum[:, b, i:i + 1])
                last.then_inc(elu_done.sem, 1)

            def one_pass(t, layer0, layer1):
                if layer0 and layer1:
                    for c in range(K):
                        wait(act, hop_mm, t - 1, K + c)
                        act.dma_start(xt_sb[:, c], xt[t][:, c]).then_inc(xt_in[c].sem, 16)
                if layer1:
                    for c in range(K):
                        wait(act, tr_mm, t, c)
                        nc.scalar.copy(ring[:, XT_TILE:XT_TILE + PAIR, c * P:(c + 1) * P],
                                       misc_ps[:, c % MB, 0:PAIR * P].rearrange("p (b q) -> p b q", b=PAIR)
                                       ).then_inc(xt_ev.sem, 1)
                    for i in range(K):
                        b, half = divmod(i, K // 2)
                        wait(act, h_mm, t, i)
                        nc.scalar.copy(haug[:, b, 2 * half:2 * half + 2, 1:HW],
                                       misc_ps[:, (K + i) % MB, :].rearrange("p (e n) -> p e n", e=2)[:, :, 0:F + 2]
                                       ).then_inc(h_ev.sem, 1)
                if layer0:
                    for c in range(K):
                        copy_y_hi(t, c)
                for slot in range(SLOTS):
                    if layer1:
                        for s in STEPS_IN.get(slot, []):
                            if s == 0:
                                second_branch(t, 0)
                            if s + 1 < STEPS and s != K - 1:
                                second_branch(t, s + 1)
                            if s == K:
                                pass
                            exp(t, s)
                            if s == K - 1:
                                second_branch(t, K)
                        if slot == EPI_SLOT:
                            elu_parts(t, 0)
                    if layer0 and slot < K:
                        copy_z_hi(t, slot)
                if layer1:
                    elu_parts(t, 1)

            passes(act, one_pass)

        @block.tensor
        def _(pe):
            pe.wait_ge(consts_in, 16 * 7)
            nc.tensor.matmul(misc_ps[:, 0, 0:2], xres[:, 1, 0, :], xres[:, 1, 1, 0:2], start=True, stop=True).then_inc(wa_mm, 1)
            pe.wait_ge(theta_done, 3)
            pe.wait_ge(w_done, 1)

            def transpose_x(t, c):
                wait(pe, xn_done, t - 1, c)
                misc_free(pe, t, c, False)
                for b in range(PAIR):
                    mm = nc.tensor.transpose(misc_ps[:, c % MB, b * P:(b + 1) * P], xn[:, b, c, :], ident[:])
                mm.then_inc(tr_mm.sem, 1)

            def project_h(t, i):
                b, half = divmod(i, K // 2)
                wait(pe, xt_ev, t, 2 * half + 1)
                misc_free(pe, t, K + i, False)
                for e in range(2):
                    k = 2 * half + e
                    mm = nc.tensor.matmul(misc_ps[:, (K + i) % MB, e * 256:e * 256 + F + 2],
                                          ring[:, XT_TILE + b, k * P:(k + 1) * P], w_aug[:], start=True, stop=True)
                mm.then_inc(h_mm.sem, 1)

            def project_y(t, c, layer1):
                pos = 2 * K + c
                wait(pe, xt_in[c], t, 0)
                if layer1 or c >= MB:
                    misc_free(pe, t, pos, not layer1)
                for b in range(PAIR):
                    mm = nc.tensor.matmul(misc_ps[:, pos % MB, b * F:(b + 1) * F], xt_sb[:, c, b, :], t24[:],
                                          start=True, stop=True)
                mm.then_inc(y_mm.sem, 1)

            def hop(t, slot):
                second, c = divmod(slot, K)
                hi, lo = (z_hi, z_lo) if second else (y_hi, y_lo)
                th = t0 if second else t13
                if c == 0:
                    wait(pe, z_lo_done if second else y_lo_done, t, K - 1)
                prev = slot - HB
                if prev >= K:
                    wait(pe, x1_done, t, prev - K)
                elif prev >= 0:
                    wait(pe, z_lo_done, t, prev)
                elif not (isinstance(t, int) and t == 0):
                    wait(pe, x1_done, t - 1, prev + K)
                dst = hop_ps[:, slot % HB, 0:PAIR * F]
                for k in range(K):
                    if isinstance(t, int) and slot == 0:
                        pe.wait_ge(a_lo_done, k + 1)
                        pe.wait_ge(a_hi_done, k + 1)
                    for n, (sta, mov) in enumerate(((a_hi, hi), (a_hi, lo), (a_lo, hi))):
                        last = k == K - 1 and n == 2
                        if last:
                            for b in range(PAIR):
                                nc.tensor.matmul(dst[:, b * F:(b + 1) * F], xt_sb[:, c, b, :], th[:],
                                                 start=False, stop=False)
                            if second:
                                nc.tensor.matmul(dst, ones[:], bias_r[:], start=False, stop=False)
                        mm = nc.tensor.matmul(dst, sta[:, k, c * P:(c + 1) * P], mov[:, k, :],
                                              start=(k == 0 and n == 0), stop=last)
                mm.then_inc(hop_mm.sem, 1)

            def pv(t, s):
                b, k = divmod(s, K)
                wait(pe, p_done, t, s)
                if s == K:
                    wait(pe, elu_done, t, 0)
                for i in range(K):
                    bank, at = divmod(i, PV_PER_BANK)
                    mm = nc.tensor.matmul(pv_ps[:, bank, at * PVW:(at + 1) * PVW],
                                          ring[:, s % RING, i * P:(i + 1) * P], haug[:, b, k, 0:PVW],
                                          start=(k == 0 and at == 0), stop=(k == K - 1), skip_group_check=True)
                mm.then_inc(pv_mm.sem, 1)

            def one_pass(t, layer0, layer1):
                if layer1:
                    for c in range(K):
                        transpose_x(t, c)
                    for i in range(K):
                        project_h(t, i)
                if layer0:
                    for c in range(K):
                        project_y(t, c, layer1)
                for slot in range(SLOTS):
                    if layer0:
                        hop(t, slot)
                    if layer1:
                        for s in STEPS_IN.get(slot - 1, []):
                            pv(t, s)
                if layer1:
                    for s in STEPS_IN[SLOTS - 1]:
                        pv(t, s)

            passes(pe, one_pass)

        @block.vector
        def _(dve):
            v = nc.vector
            chain = [0]

            def link(ins):
                chain[0] += 1
                ins.then_inc(dve_setup, 1)
                dve.wait_ge(dve_setup, chain[0])

            dve.wait_ge(theta_in, 16)
            th = xres[:, 0]
            link(v.tensor_tensor(t24[:], th[:, 2, :], th[:, 4, :], ALU.add))
            v.tensor_tensor(t0[:], th[:, 0, :], t24[:], ALU.subtract).then_inc(theta_done, 1)
            v.tensor_tensor(t13[:], th[:, 1, :], th[:, 3, :], ALU.add).then_inc(theta_done, 1)
            dve.wait_ge(theta_done, 2)
            v.tensor_scalar(t24[:], t24[:], 2.0, None, ALU.mult).then_inc(theta_done, 1)
            dve.wait_ge(consts_in, 16 * 7)
            link(v.memset(haug[:, :, :, 0:1], 1.0))
            link(v.memset(xres[:, 1, 3, :], 1.0))
            link(v.tensor_copy(ones[:], xres[:, 1, 3, :]))
            link(v.memset(xres[:, 1, 4, :], 0.0))
            link(v.tensor_copy(bias_r[:, 0:F], xres[:, 1, 4, :]))
            link(v.tensor_copy(bias_r[:, F:2 * F], xres[:, 1, 4, :]))
            two = slice(0, 2)
            link(v.tensor_copy(bias_r[two, 0:F], xres[two, 1, 2, :]))
            link(v.tensor_tensor(xres[two, 1, 3, :], xres[two, 1, 2, :], bias_r[two, 0:F].bitcast(F32), ALU.subtract))
            link(v.tensor_scalar(xres[two, 1, 4, :], bias_r[two, 0:F].bitcast(F32), ident[two, 0:1], None, ALU.mult))
            for b in range(PAIR):
                link(v.scalar_tensor_tensor(bias_r[two, b * F:(b + 1) * F], xres[two, 1, 3, :], ident[two, 1:2],
                                            xres[two, 1, 4, :], ALU.mult, ALU.add))

            def split_a(k):
                dve.wait_ge(a_in[k], 16)
                v.tensor_scalar(neg[:, k, :], ring[:, k, :], 0.0, MASKED, ALU.is_le, ALU.mult).then_inc(dve_setup, 1)
                chain[0] += 1
                dve.wait_ge(a_hi_done, k + 1)
                v.tensor_tensor(a_lo[:, k, :], ring[:, k, :], a_hi[:, k, :].bitcast(F32), ALU.subtract).then_inc(a_lo_done, 1)
                diag = ring[:, k, k * P:(k + 1) * P]
                dve.wait_ge(a_lo_done, k + 1)
                link(v.tensor_tensor(diag, diag, ident[:], ALU.add))
                v.tensor_scalar(neg[:, k, k * P:(k + 1) * P], diag, 0.0, MASKED, ALU.is_le, ALU.mult).then_inc(neg_done, 1)

            def mask_of(k):
                dve.wait_ge(at_in[k], 16)
                link(v.tensor_scalar(mask_t[:, k, :], ring[:, k, :], 0.0, None, ALU.is_gt))
                diag = ring[:, k, k * P:(k + 1) * P]
                link(v.tensor_tensor(diag, diag, ident[:], ALU.add))
                v.tensor_scalar(mask_t[:, k, k * P:(k + 1) * P], diag, 0.0, None, ALU.is_gt).then_inc(mask_done, 1)

            def sub_y_lo(t, c):
                wait(dve, y_hi_done, t, c)
                v.tensor_tensor(y_lo[:, c, :], misc_ps[:, (2 * K + c) % MB, 0:PAIR * F], y_hi[:, c, :].bitcast(F32),
                                ALU.subtract).then_inc(y_lo_done.sem, 1)

            def sub_z_lo(t, c):
                wait(dve, z_hi_done, t, c)
                v.tensor_tensor(z_lo[:, c, :], hop_ps[:, c % HB, 0:PAIR * F], z_hi[:, c, :].bitcast(F32),
                                ALU.subtract).then_inc(z_lo_done.sem, 1)

            def residual0(t, c):
                if c == 0:
                    wait(dve, x_in, t, 0)
                wait(dve, hop_mm, t, K + c)
                v.scalar_tensor_tensor(xn[:, :, c, :], hop_ps[:, c % HB, 0:PAIR * F].rearrange("p (b f) -> p b f", b=PAIR),
                                       0.0, xn[:, :, c, :], ALU.max, ALU.add).then_inc(x1_done.sem, 1)
                wait(dve, x1_done, t, c)
                for b in range(PAIR):
                    last = v.bn_stats(stats1[:, b, :], xn[:, b, c, :])
                last.then_inc(bn1_done.sem, 1)
                wait(dve, bn1_done, t, c, theta_done)
                for b in range(PAIR):
                    last = v.bn_aggr(mv1[:, c, b, :], stats1[:, b, :])
                last.then_inc(mv1_done.sem, 1)

            def normalise0(t, c):
                wait(dve, rstd1_done, t, c)
                for b in range(PAIR):
                    last = v.tensor_scalar(xn[:, b, c, :], xn[:, b, c, :], mv1[:, c, b, 0:1], rstd1[:, c, b:b + 1],
                                           ALU.subtract, ALU.mult)
                last.then_inc(xn_done.sem, 1)

            def d_columns(t, b):
                wait(dve, h_ev, t, (b + 1) * K // 2 - 1)
                v.tensor_copy(d_col[:, b, :], haug[:, b, :, F + 2])
                v.tensor_scalar(d02[:, b, :], haug[:, b, :, F + 2], ALPHA, None, ALU.mult).then_inc(d_ready.sem, 1)

            def masked_max(t, b, k):
                if k == 0:
                    wait(dve, d_in[b], t, 0, theta_done)
                v.tensor_tensor_reduce(ring[:, JUNK_TILE, :].rearrange("p (k q) -> p k q", k=K),
                                       neg[:, k, :].rearrange("p (k q) -> p k q", k=K),
                                       ring[:, D_TILE + b, :].rearrange("p (q k) -> p k q", k=K),
                                       1.0, 4 * MASKED, ALU.add, ALU.max, dmax[:, k:k + 1]).then_inc(max_done.sem, 1)
                wait(dve, max_done, t, b * K + k, theta_done)

            def ab_columns(t, b):
                s = haug[:, b, :, F + 1]
                v.tensor_tensor(logit[:], s, dmax[:], ALU.add).then_inc(logit_done.sem, 1)
                wait(dve, logit_done, t, b)
                v.scalar_tensor_tensor(m_col[:], logit[:], ALPHA, logit[:], ALU.mult, ALU.max).then_inc(m_done.sem, 1)
                wait(dve, m_done, t, b)
                v.tensor_tensor(ab_col[:, b, 0, :], s, m_col[:], ALU.subtract)
                v.scalar_tensor_tensor(ab_col[:, b, 1, :], s, ALPHA, m_col[:], ALU.mult, ALU.subtract).then_inc(ab_ready.sem, 1)

            def exponent(t, s):
                b, k = divmod(s, K)
                if k == 0:
                    wait(dve, ab_in[b], t, 0)
                wait(dve, t2_done, t, s)
                tile = ring[:, s % RING, :].rearrange("p (k q) -> p k q", k=K)
                v.scalar_tensor_tensor(tile, rows_ab[:, b].rearrange("p a n -> p (a n)").rearrange("p (q a k) -> p a k q", a=2, k=K)[:, 0],
                                       haug[:, b, k, F + 2:F + 3], tile, ALU.add, ALU.max).then_inc(z_done.sem, 1)

            def mask_p(t, s):
                wait(dve, exp_done, t, s)
                v.scalar_tensor_tensor(ring[:, s % RING, :], ring[:, s % RING, :], 1.0, mask_t[:, s % K, :],
                                       ALU.min, ALU.mult).then_inc(p_done.sem, 1)

            def row_sums(t, b):
                wait(dve, pv_mm, t, (b + 1) * K - 1)
                for bank in range(PV_BANKS):
                    lo, hi = bank * PV_PER_BANK, min(K, (bank + 1) * PV_PER_BANK)
                    last = v.reciprocal(rsum[:, b, lo:hi], pv_ps[:, bank, 0:(hi - lo - 1) * PVW + 1:PVW])
                last.then_inc(rsum_done.sem, 1)

            def residual1(t, b):
                wait(dve, elu_done, t, b)
                wait(dve, xres_in, t, PAIR - 1)
                y = xres[:, b].rearrange("p k f -> p (k f)")
                v.scalar_tensor_tensor(y, rows_ab[:, b, 1, :], 1.0, y, ALU.min, ALU.add).then_inc(w_sum.sem, 1)
                wait(dve, w_sum, t, b)
                v.scalar_tensor_tensor(y, rows_ab[:, b, 0, :], -1.0, y, ALU.add, ALU.add).then_inc(y_done.sem, 1)
                wait(dve, y_done, t, b)
                for k in range(K):
                    last = v.bn_stats(stats2[:, k, :], xres[:, b, k, :])
                last.then_inc(bn2_done.sem, 1)
                wait(dve, bn2_done, t, b, theta_done)
                for k in range(K):
                    last = v.bn_aggr(mv2[:, k, :], stats2[:, k, :])
                last.then_inc(mv2_done.sem, 1)

            def normalise1(t, b):
                wait(dve, rstd2_done, t, b)
                for k in range(K):
                    last = v.tensor_scalar(xres[:, b, k, :], xres[:, b, k, :], mv2[:, k, 0:1], rstd2[:, k:k + 1],
                                           ALU.subtract, ALU.mult)
                last.then_inc(out_done.sem, 1)

            for k in range(K):
                split_a(k)

            def one_pass(t, layer0, layer1):
                if layer1:
                    for b in range(PAIR):
                        d_columns(t, b)
                if layer0:
                    for c in range(K):
                        sub_y_lo(t, c)
                if layer0 and not layer1:
                    for k in range(K):
                        mask_of(k)
                for slot in range(SLOTS):
                    if layer1:
                        if slot in MAXES:
                            b, blocks = MAXES[slot]
                            for k in blocks:
                                masked_max(t, b, k)
                            if blocks[-1] == K - 1:
                                ab_columns(t, b)
                        for s in STEPS_IN.get(slot, []):
                            exponent(t, s)
                            if s % K:
                                mask_p(t, s - 1)
                            if s % K == K - 1:
                                mask_p(t, s)
                        if slot == EPI_SLOT:
                            row_sums(t, 0)
                            residual1(t, 0)
                        if slot == EPI_SLOT + 1:
                            normalise1(t, 0)
                    if layer0:
                        if slot < K:
                            sub_z_lo(t, slot)
                        else:
                            residual0(t, slot - K)
                            if slot > K:
                                normalise0(t, slot - K - 1)
                if layer0:
                    normalise0(t, K - 1)
                if layer1:
                    row_sums(t, 1)
                    residual1(t, 1)
                    normalise1(t, 1)

            passes(dve, one_pass)


def kernel(**inputs):
    import numpy as np
    import concourse.bacc as bacc
    from concourse.bass_utils import run_bass_kernel_spmd

    x, adj = np.asarray(inputs["x"]), np.asarray(inputs["adj"])
    theta, w = np.asarray(inputs["L0_gnn_Theta1"]), np.asarray(inputs["L1_gnn_W"])
    blocks = theta.shape[0] // F
    by_block = lambda a: a.reshape(P, K, P, K).transpose(0, 1, 3, 2).reshape(P, K, N)
    laid = {
        "x": x.reshape(GROUPS, PAIR, P, K, F).transpose(0, 2, 1, 3, 4),
        "xt": x.reshape(GROUPS, PAIR, P, K, F).transpose(0, 4, 3, 1, 2),
        "adj": by_block(adj),
        "adjt": by_block(adj.T),
        "theta": theta.reshape(blocks, F, F).transpose(1, 0, 2),
        "bias": np.asarray(inputs["L0_gnn_bias"]).reshape(1, F),
        "w": w,
        "wt": w.T,
        "a_src": np.asarray(inputs["L1_gnn_a_src"]),
        "a_dst": np.asarray(inputs["L1_gnn_a_dst"]),
        "ident_in": np.eye(P, dtype=np.float32),
    }
    laid = {name: np.ascontiguousarray(a) for name, a in laid.items()}
    nc = bacc.Bacc("TRN2", target_bir_lowering=False, num_devices=1)
    aps = {name: nc.dram_tensor(f"in_{name}", a.shape, mybir.dt.from_np(a.dtype), kind="ExternalInput").ap()
           for name, a in laid.items()}
    out = nc.dram_tensor("out_0", [GROUPS, P, PAIR, K, F], F32, kind="ExternalOutput").ap()
    chebyshev_then_attention(nc, out=out, **aps)
    r = run_bass_kernel_spmd(nc, [{f"in_{name}": a for name, a in laid.items()}], core_ids=[0])
    got = np.asarray(r.results[0]["out_0"])
    return got.reshape(GROUPS, P, PAIR, K, F).transpose(0, 2, 1, 3, 4).reshape(B, N, F)
```

```python
from contextlib import ExitStack

import concourse.bass as bass
from concourse import mybir

F32, F32R, BF16, U8 = mybir.dt.float32, mybir.dt.float32r, mybir.dt.bfloat16, mybir.dt.uint8
ALU = mybir.AluOpType
ACT = mybir.ActivationFunctionType

P = 128
B, N, F = 8, 1024, 128
K = N // P
PAIR = 2
GROUPS = B // PAIR
SLOTS = 2 * K
STEPS = PAIR * K
RING = 8
HB, MB = 2, 3
FIRST = HB + 3
BANK = 512
HW = F + 3
PVW = F + 1
PV_PER_BANK = BANK // PVW
PV_BANKS = -(-K // PV_PER_BANK)
ALPHA, EPS, MASKED = 0.2, 1e-5, -1e30
XT_TILE, D_TILE = 0, (2, 7)

BESIDE_LAYER0 = dict(
    maxes={0: (0, (0,)), 1: (0, (1, 2, 3)), 2: (0, (4, 5, 6, 7)),
           8: (1, (0, 1)), 9: (1, (2, 3)), 10: (1, (4, 5)), 11: (1, (6, 7))},
    steps={5: (0,), 6: (1,), 8: (2,), 9: (3,), 10: (4, 5), 11: (6,), 12: (7,), 13: (8,), 14: (9,)},
    products={8: (0,), 9: (1,), 10: (2,), 11: (3, 4), 12: (5,), 13: (6, 7)},
    sums=14, old_out=6, old_moments=7)
ALONE = dict(
    maxes={3: (0, (0, 1, 2, 3)), 4: (0, (4, 5, 6, 7)), 6: (1, (0, 1)), 7: (1, (2, 3)), 8: (1, (4, 5)), 9: (1, (6, 7))},
    steps={6: (0,), 7: (1,), 8: (2,), 9: (3,), 10: (4,), 11: (5,), 12: (6,), 13: (7,), 14: (8, 9)},
    products={7: (0,), 8: (1,), 9: (2,), 10: (3,), 11: (4,), 12: (5,), 13: (6,), 14: (7,)},
    sums=15, old_out=4, old_moments=5)
OLD_PV_IN = {0: (11,), 1: (12, 13), 2: (14,), 3: (15,)}
POOL_BLOCKS = (1, 3, 5)
MADE, MULTIPLIED = 10, 8
H1_SLOT = 4
OLD_SUMS_SLOT = 4


def on_pool(s):
    return s % K in POOL_BLOCKS


def nth(s):
    return sum(on_pool(e) == on_pool(s) for e in range(s))


class Signal:

    def __init__(self, sem, per, first, unit=1):
        self.sem, self.per, self.first, self.unit = sem, per, first, unit

    def level(self, t, i):
        return (t - self.first) * (self.per * self.unit) + (i + 1) * self.unit


def wait(eng, signal, t, i, up=None):
    level = signal.level(t, i)
    if up is not None:
        if not isinstance(level, int):
            register = eng.alloc_register()
            eng.reg_mov(register, level)
            level = register
        eng.wait_ge(up, 1)
    eng.wait_ge(signal.sem, level)
    if up is not None and not isinstance(level, int):
        eng.free_register(level)


def chebyshev_then_attention(nc, x, xt, adj, adjt, theta, bias, w, wt, a_src, a_dst, ident_in, out):
    with ExitStack() as ctx:
        def sb(name, shape, dt=F32):
            return ctx.enter_context(nc.sbuf_tensor(name, shape, dt))

        def sem(name):
            return ctx.enter_context(nc.semaphore(name))

        a_hi = sb("a_hi", [P, K, N], F32R)
        a_lo = sb("a_lo", [P, K, N], F32R)
        neg = sb("neg", [P, K, N], BF16)
        mask_t = sb("mask_t", [P, K - len(POOL_BLOCKS), N], U8)
        neg_t = sb("neg_t", [P, len(POOL_BLOCKS), N], BF16)
        y_hi = sb("y_hi", [P, K, PAIR * F], F32R)
        y_lo = sb("y_lo", [P, K, PAIR * F], F32R)
        z_hi = sb("z_hi", [P, K, PAIR * F], F32R)
        z_lo = sb("z_lo", [P, K, PAIR * F], F32R)
        xt_sb = sb("xt_sb", [P, K, PAIR, P])
        xn = sb("xn", [P, PAIR, K, F])
        xres = sb("xres", [P, PAIR, K, F])
        haug = sb("haug", [P, PAIR, K, HW])
        rows_ab = sb("rows_ab", [P, PAIR, 2, N])
        ring = sb("ring", [P, RING, N])
        ident = sb("ident", [P, P])
        t24 = sb("t24", [P, F])
        t13 = sb("t13", [P, F])
        t0 = sb("t0", [P, F])
        w_aug = sb("w_aug", [P, F + 2])
        ones = sb("ones", [P, P], F32R)
        bias_r = sb("bias_r", [P, F], F32R)
        minus_half = sb("minus_half", [P, K])
        stats1 = sb("stats1", [P, PAIR, 6])
        mv1 = sb("mv1", [P, K, PAIR, 2])
        rstd1 = sb("rstd1", [P, K, PAIR])
        nmr1 = sb("nmr1", [P, K, PAIR])
        stats2 = sb("stats2", [P, K, 6])
        mv2 = sb("mv2", [P, PAIR, K, 2])
        rstd2 = sb("rstd2", [P, PAIR, K])
        nmr2 = sb("nmr2", [P, PAIR, K])
        d_col = sb("d_col", [P, PAIR, K])
        d02 = sb("d02", [P, PAIR, K])
        dmax = sb("dmax", [P, K])
        ab_col = sb("ab_col", [P, PAIR, 2, K])
        rsum = sb("rsum", [P, PAIR, K])
        hop_ps = ctx.enter_context(nc.psum_tensor("hop_ps", [P, HB, BANK], F32))
        misc_ps = ctx.enter_context(nc.psum_tensor("misc_ps", [P, MB, BANK], F32))
        pv_ps = ctx.enter_context(nc.psum_tensor("pv_ps", [P, PV_BANKS, BANK], F32))
        d_row = nc.dram_tensor("d_row", [PAIR, P, K], F32, kind="Internal").ap()
        ab_row = nc.dram_tensor("ab_row", [PAIR, 2, P, K], F32, kind="Internal").ap()

        consts_in, theta_in = sem("consts_in"), sem("theta_in")
        a_in = [sem(f"a_in{k}") for k in range(K)]
        at_in = [sem(f"at_in{k}") for k in range(K)]
        a_hi_done, a_lo_done, neg_done, mask_done = sem("a_hi_done"), sem("a_lo_done"), sem("neg_done"), sem("mask_done")
        theta_done, wa_mm, w_done, half_done, bias_done, dve_setup = (
            sem("theta_done"), sem("wa_mm"), sem("w_done"), sem("half_done"), sem("bias_done"), sem("dve_setup"))
        xt_in = [Signal(sem(f"xt_in{c}"), 1, 0, 16) for c in range(K)]
        x_in = Signal(sem("x_in"), 1, 0, 16)
        y_mm, y_hi_done, y_lo_done = (Signal(sem(s), K, 0) for s in ("y_mm", "y_hi_done", "y_lo_done"))
        hop_mm = Signal(sem("hop_mm"), SLOTS, 0)
        z_hi_done, z_lo_done = (Signal(sem(s), K, 0) for s in ("z_hi_done", "z_lo_done"))
        x1_done, bn1_done, mv1_done, eps1_done, rstd1_done, nmr1_done, xn_done = (
            Signal(sem(s), K, 0) for s in ("x1_done", "bn1_done", "mv1_done", "eps1_done", "rstd1_done", "nmr1_done", "xn_done"))
        tr_mm, xt_ev, h_mm, h_ev = (Signal(sem(s), K, 0) for s in ("tr_mm", "xt_ev", "h_mm", "h_ev"))
        xres_in = [Signal(sem(f"xres_in{b}"), 1, 0, 16) for b in range(PAIR)]
        d_ready, ab_ready = (Signal(sem(s), PAIR, 0) for s in ("d_ready", "ab_ready"))
        d_out, ab_out = (Signal(sem(s), PAIR, 0, 16) for s in ("d_out", "ab_out"))
        d_in = [Signal(sem(f"d_in{b}"), 1, 0, 16) for b in range(PAIR)]
        a_row_in = [Signal(sem(f"a_row_in{b}"), 1, 0, 16) for b in range(PAIR)]
        b_row_in = [Signal(sem(f"b_row_in{b}"), 1, 0, 16) for b in range(PAIR)]
        max_done, logit_done, m_done = Signal(sem("max_done"), STEPS, 0), Signal(sem("logit_done"), PAIR, 0), Signal(sem("m_done"), PAIR, 0)
        t2_done, z_done, pv_mm = (
            Signal(sem(s), STEPS, 0) for s in ("t2_done", "z_done", "pv_mm"))
        on_dve = STEPS - PAIR * len(POOL_BLOCKS)
        exp_done = (Signal(sem("exp_done"), on_dve, 0), Signal(sem("masked_exp_done"), STEPS - on_dve, 0))
        zm_done, p_done = Signal(sem("zm_done"), STEPS - on_dve, 0), Signal(sem("p_done"), on_dve, 0)
        rsum_done, elu_done, w_sum, y_done, bn2_done, mv2_done, eps2_done, rstd2_done, nmr2_done, out_done = (
            Signal(sem(s), PAIR, 0) for s in
            ("rsum_done", "elu_done", "w_sum", "y_done", "bn2_done", "mv2_done", "eps2_done", "rstd2_done", "nmr2_done", "out_done"))
        out_stored = [Signal(sem(f"out_stored{b}"), 1, 0, 16) for b in range(PAIR)]

        def passes(eng, one_pass):
            one_pass(0, True, False, False)
            one_pass(1, True, True, False)
            with eng.Fori(2, GROUPS) as t:
                one_pass(t, True, True, True)
            one_pass(GROUPS, False, True, True)
            one_pass(GROUPS + 1, False, False, True)

        def misc_free(eng, t, pos, layer0):
            prev = pos - MB
            if prev >= 2 * K:
                wait(eng, h_ev, t - 1, prev - 2 * K)
            elif prev >= K:
                wait(eng, xt_ev, t - 1, prev - K)
            elif prev >= 0 and layer0:
                wait(eng, y_lo_done, t, prev)

        def hop_bank(t, slot):
            if isinstance(t, int) and t == 0 and HB <= slot < FIRST:
                return pv_ps[:, slot - HB, 0:PAIR * F]
            return hop_ps[:, slot % HB, 0:PAIR * F]

        block = ctx.enter_context(nc.Block())

        @block.sync
        def _(sp):
            for c in range(1, K, 2):
                sp.dma_start(xt_sb[:, c], xt[0][:, c]).then_inc(xt_in[c].sem, 16)
            for k in range(K):
                sp.dma_start(ring[:, k, :], adj[:, k, :]).then_inc(a_in[k], 16)
            for dst, src in ((ident[:], ident_in), (w_aug[:, 0:F], w)):
                sp.dma_start(dst, src).then_inc(consts_in, 16)
            sp.dma_start(xres[:, 1, 0, :], wt).then_inc(consts_in, 16)
            sp.dma_start(xres[:, 1, 1, 0:1], a_src).then_inc(consts_in, 16)
            sp.dma_start(xres[:, 1, 1, 1:2], a_dst).then_inc(consts_in, 16)
            sp.dma_start(xres[0:1, 1, 2, :], bias).then_inc(consts_in, 16)
            sp.dma_start(xres[1:2, 1, 2, :], bias).then_inc(consts_in, 16)
            sp.dma_start(xn[:], x[0]).then_inc(x_in.sem, 16)
            for k in range(K):
                sp.wait_ge(a_hi_done, k + 1)
                sp.wait_ge(a_lo_done, k + 1)
                sp.wait_ge(neg_done, k + 1)
                sp.dma_start(ring[:, k, :], adjt[:, k, :]).then_inc(at_in[k], 16)

            def d_to_dram(u, b):
                wait(sp, d_ready, u, b)
                sp.dma_start(d_row[b], d_col[:, b, :]).then_inc(d_out.sem, 16)

            def d_to_all(u, b):
                wait(sp, d_out, u, b)
                sp.dma_start(ring[:, D_TILE[b], :],
                             d_row[b].rearrange("(o p) k -> o (p k)", o=1).broadcast_to([P, N])).then_inc(d_in[b].sem, 16)

            def ab_to_dram(u, b):
                wait(sp, ab_ready, u, b)
                sp.dma_start(ab_row[b].rearrange("a p k -> p a k"), ab_col[:, b]).then_inc(ab_out.sem, 16)

            def ab_to_all(u, b, old):
                if old:
                    wait(sp, out_stored[b], u - 1, 0, theta_done)
                wait(sp, ab_out, u, b)
                for a, signal in ((1, b_row_in), (0, a_row_in)):
                    sp.dma_start(rows_ab[:, b, a], ab_row[b, a].rearrange("(o p) k -> o (p k)", o=1).broadcast_to([P, N])
                                 ).then_inc(signal[b].sem, 16)

            def x_to_residual(u, b, old):
                if old:
                    wait(sp, y_done, u - 1, b, theta_done)
                wait(sp, xn_done, u, K - 1)
                sp.dma_start(xres[:, b], xn[:, b]).then_inc(xres_in[b].sem, 16)

            def one_pass(t, layer0, new, old):
                if not new:
                    return
                u = t - 1
                d_to_dram(u, 0)
                d_to_all(u, 0)
                x_to_residual(u, 0, old)
                if not layer0:
                    d_to_dram(u, 1)
                    d_to_all(u, 1)
                ab_to_dram(u, 0)
                ab_to_all(u, 0, old)
                if layer0:
                    d_to_dram(u, 1)
                    d_to_all(u, 1)
                x_to_residual(u, 1, old)
                if layer0:
                    for b in range(PAIR):
                        wait(sp, xres_in[b], u, 0, theta_done)
                    wait(sp, tr_mm, u, K - 1)
                    sp.dma_start(xn[:], x[t]).then_inc(x_in.sem, 16)
                ab_to_dram(u, 1)
                ab_to_all(u, 1, old)

            passes(sp, one_pass)
            for b in range(PAIR):
                wait(sp, out_stored[b], GROUPS - 1, 0)

        @block.gpsimd
        def _(pool):
            nc.gpsimd.memset(minus_half[:], -0.5).then_inc(half_done, 1)
            pool.wait_ge(half_done, 1)

            def rstd1_of(t, c):
                wait(pool, mv1_done, t, c, half_done)
                nc.gpsimd.tensor_scalar(rstd1[:, c, :], mv1[:, c, :, 1], EPS, 1.0, ALU.add, ALU.mult)
                nc.gpsimd.tensor_scalar(nmr1[:, c, :], mv1[:, c, :, 0], -1.0, 0.0, ALU.mult, ALU.add).then_inc(eps1_done.sem, 1)
                wait(pool, eps1_done, t, c)
                nc.gpsimd.tensor_tensor(rstd1[:, c, :], rstd1[:, c, :], minus_half[:, 0:PAIR], ALU.pow).then_inc(rstd1_done.sem, 1)
                wait(pool, rstd1_done, t, c)
                nc.gpsimd.tensor_tensor(nmr1[:, c, :], nmr1[:, c, :], rstd1[:, c, :], ALU.mult).then_inc(nmr1_done.sem, 1)

            def norm2_of(t, b):
                wait(pool, mv2_done, t, b, half_done)
                nc.gpsimd.tensor_scalar(rstd2[:, b], mv2[:, b, :, 1], EPS, 1.0, ALU.add, ALU.mult)
                nc.gpsimd.tensor_scalar(nmr2[:, b], mv2[:, b, :, 0], -1.0, 0.0, ALU.mult, ALU.add).then_inc(eps2_done.sem, 1)
                wait(pool, eps2_done, t, b)
                nc.gpsimd.tensor_tensor(rstd2[:, b], rstd2[:, b], minus_half[:, 0:K], ALU.pow).then_inc(rstd2_done.sem, 1)
                wait(pool, rstd2_done, t, b)
                nc.gpsimd.tensor_tensor(nmr2[:, b], nmr2[:, b], rstd2[:, b], ALU.mult).then_inc(nmr2_done.sem, 1)

            def store(t, b):
                wait(pool, out_done, t, b, half_done)
                pool.dma_start(out[t][:, b], rows_ab[:, b, 0, :].rearrange("p (k f) -> p k f", k=K)).then_inc(out_stored[b].sem, 16)

            def mask_z(t, s):
                if on_pool(s):
                    wait(pool, z_done, t, s)
                    nc.gpsimd.tensor_tensor(ring[:, s % RING, :], ring[:, s % RING, :], neg_t[:, nth(s % K), :],
                                            ALU.add).then_inc(zm_done.sem, 1)

            def one_pass(t, layer0, new, old):
                u, o = t - 1, t - 2
                plan = BESIDE_LAYER0 if layer0 else ALONE
                if old:
                    mask_z(o, 11)
                    mask_z(o, 13)
                    norm2_of(o, 0)
                    store(o, 0)
                for slot in range(SLOTS):
                    if old and slot == plan["old_moments"] + 1:
                        norm2_of(o, 1)
                    if new:
                        for s in plan["steps"].get(slot, ()):
                            mask_z(u, s)
                    if old and slot == plan["old_moments"] + 2:
                        store(o, 1)
                    if layer0 and slot >= K:
                        rstd1_of(t, slot - K)

            passes(pool, one_pass)

        @block.scalar
        def _(act):
            act.dma_start(xres[:, 0, 0:5, :], theta).then_inc(theta_in, 16)
            for c in range(0, K, 2):
                act.dma_start(xt_sb[:, c], xt[0][:, c]).then_inc(xt_in[c].sem, 16)

            def split_a_hi(k):
                act.wait_ge(a_in[k], 16)
                nc.scalar.copy(a_hi[:, k, :], ring[:, k, :]).then_inc(a_hi_done, 1)

            def copy_y_hi(t, c):
                wait(act, y_mm, t, c)
                if not (isinstance(t, int) and t == 0):
                    wait(act, hop_mm, t - 1, K - 1)
                nc.scalar.copy(y_hi[:, c, :], misc_ps[:, c % MB, 0:PAIR * F]).then_inc(y_hi_done.sem, 1)

            def copy_z_hi(t, c):
                wait(act, hop_mm, t, c)
                if not (isinstance(t, int) and t == 0):
                    wait(act, hop_mm, t - 1, SLOTS - 1)
                nc.scalar.copy(z_hi[:, c, :], hop_bank(t, c)).then_inc(z_hi_done.sem, 1)

            def normalise0(t, c):
                wait(act, nmr1_done, t, c)
                for b in range(PAIR):
                    last = nc.scalar.activation(xn[:, b, c, :], xn[:, b, c, :], ACT.Identity,
                                                bias=nmr1[:, c, b:b + 1], scale=rstd1[:, c, b:b + 1])
                last.then_inc(xn_done.sem, 1)

            def next_xt(t, c):
                wait(act, hop_mm, t, K + c)
                act.dma_start(xt_sb[:, c], xt[(t + 1) % GROUPS][:, c]).then_inc(xt_in[c].sem, 16)

            def second_branch(t, s, old=True):
                b, k = divmod(s, K)
                if k == 0:
                    wait(act, b_row_in[b], t, 0)
                if s == XT_TILE + 1:
                    wait(act, h_mm, t, K - 1)
                elif s == D_TILE[1]:
                    wait(act, max_done, t, STEPS - 1)
                elif s >= RING:
                    wait(act, pv_mm, t, s - RING)
                elif s >= MULTIPLIED - RING and old:
                    wait(act, pv_mm, t - 1, s + STEPS - RING)
                nc.scalar.activation(ring[:, s % RING, :].rearrange("p (k q) -> p k q", k=K),
                                     rows_ab[:, b, 1].rearrange("p (q k) -> p k q", k=K),
                                     ACT.Identity, bias=d02[:, b, k:k + 1], scale=1.0).then_inc(t2_done.sem, 1)

            def exp(t, s):
                if on_pool(s):
                    wait(act, zm_done, t, nth(s))
                else:
                    wait(act, z_done, t, s)
                nc.scalar.activation(ring[:, s % RING, :], ring[:, s % RING, :], ACT.Exp).then_inc(exp_done[on_pool(s)].sem, 1)

            def elu_parts(t, b):
                wait(act, rsum_done, t, b)
                flat = rows_ab[:, b]
                for i in range(K):
                    src = pv_ps[:, i // PV_PER_BANK, (i % PV_PER_BANK) * PVW + 1:(i % PV_PER_BANK + 1) * PVW]
                    nc.scalar.activation(flat[:, 0, i * F:(i + 1) * F], src, ACT.Relu, scale=rsum[:, b, i:i + 1])
                    last = nc.scalar.activation(flat[:, 1, i * F:(i + 1) * F], src, ACT.Exp, scale=rsum[:, b, i:i + 1])
                last.then_inc(elu_done.sem, 1)

            def copy_xt(u, c):
                wait(act, tr_mm, u, c)
                nc.scalar.copy(ring[:, XT_TILE:XT_TILE + PAIR, c * P:(c + 1) * P],
                               misc_ps[:, (K + c) % MB, 0:PAIR * P].rearrange("p (b q) -> p b q", b=PAIR)).then_inc(xt_ev.sem, 1)

            def copy_h(u, i):
                b, half = divmod(i, K // 2)
                wait(act, h_mm, u, i)
                nc.scalar.copy(haug[:, b, 2 * half:2 * half + 2, 1:HW],
                               misc_ps[:, (2 * K + i) % MB, :].rearrange("p (e n) -> p e n", e=2)[:, :, 0:F + 2]
                               ).then_inc(h_ev.sem, 1)

            def make(u, plan, slot, old):
                for s in plan["steps"].get(slot, ()):
                    if s == 0:
                        second_branch(u, 0, old)
                    if s + 1 < K:
                        second_branch(u, s + 1, old)
                    if not on_pool(s):
                        exp(u, s)
                    if s + 1 >= K:
                        second_branch(u, s + 1, old)

            def normalise1(t, b):
                wait(act, nmr2_done, t, b)
                for k in range(K):
                    y = rows_ab[:, b, 0, k * F:(k + 1) * F]
                    last = nc.scalar.activation(y, y, ACT.Identity, bias=nmr2[:, b, k:k + 1], scale=rstd2[:, b, k:k + 1])
                last.then_inc(out_done.sem, 1)

            def one_pass(t, layer0, new, old):
                u, o = t - 1, t - 2
                plan = BESIDE_LAYER0 if layer0 else ALONE
                if new and not layer0:
                    normalise0(u, K - 1)
                if layer0:
                    for c in range(K):
                        copy_y_hi(t, c)
                        if new and c == MB - 1:
                            normalise0(u, K - 1)
                        if old and c == K // 2:
                            second_branch(o, 11)
                    if not new:
                        for k in range(K):
                            split_a_hi(k)
                elif old:
                    second_branch(o, 11)
                if old:
                    exp(o, 10)
                    second_branch(o, 12)
                if new:
                    for c in range(K):
                        copy_xt(u, c)
                if old:
                    second_branch(o, 13)
                    exp(o, 11)
                    exp(o, 12)
                if new:
                    for i in range(K // 2):
                        copy_h(u, i)
                if old:
                    second_branch(o, 14)
                for slot in range(SLOTS):
                    if new and slot == H1_SLOT:
                        for i in range(K // 2, K):
                            copy_h(u, i)
                    if layer0 and slot < K:
                        copy_z_hi(t, slot)
                    if slot == K and not new and layer0:
                        act.wait_ge(wa_mm, 1)
                        nc.scalar.copy(w_aug[:, F:F + 2], pv_ps[:, 0, 0:2]).then_inc(w_done, 1)
                    if new:
                        for s in plan["steps"].get(slot - 1, ()):
                            if on_pool(s):
                                exp(u, s)
                    if old:
                        if slot == 0:
                            second_branch(o, 15)
                            exp(o, 13)
                            exp(o, 14)
                        if slot == 1:
                            exp(o, 15)
                            normalise1(o, 0)
                        if slot == OLD_SUMS_SLOT:
                            elu_parts(o, 1)
                        if slot == plan["old_moments"] + 1:
                            normalise1(o, 1)
                    if new:
                        if slot == plan["sums"]:
                            elu_parts(u, 0)
                        make(u, plan, slot, old)
                    if layer0 and slot > K:
                        next_xt(t, slot - K - 1)
                        normalise0(t, slot - K - 1)
                if layer0:
                    next_xt(t, K - 1)

            passes(act, one_pass)
            for c in range(K):
                wait(act, xt_in[c], GROUPS, 0)

        @block.tensor
        def _(pe):
            def w_a():
                pe.wait_ge(consts_in, 16 * 7)
                nc.tensor.matmul(pv_ps[:, 0, 0:2], xres[:, 1, 0, :], xres[:, 1, 1, 0:2], start=True, stop=True).then_inc(wa_mm, 1)

            pe.wait_ge(theta_done, 3)

            def transpose_x(t, c, layer0):
                wait(pe, xn_done, t - 1, c)
                misc_free(pe, t, K + c, layer0)
                for b in range(PAIR):
                    mm = nc.tensor.transpose(misc_ps[:, (K + c) % MB, b * P:(b + 1) * P], xn[:, b, c, :], ident[:])
                mm.then_inc(tr_mm.sem, 1)

            def project_h(t, i):
                b, half = divmod(i, K // 2)
                wait(pe, xt_ev, t - 1, 2 * half + 1)
                misc_free(pe, t, 2 * K + i, True)
                for e in range(2):
                    k = 2 * half + e
                    mm = nc.tensor.matmul(misc_ps[:, (2 * K + i) % MB, e * 256:e * 256 + F + 2],
                                          ring[:, XT_TILE + b, k * P:(k + 1) * P], w_aug[:], start=True, stop=True)
                mm.then_inc(h_mm.sem, 1)

            def project_y(t, c):
                wait(pe, xt_in[c], t, 0)
                misc_free(pe, t, c, True)
                for b in range(PAIR):
                    mm = nc.tensor.matmul(misc_ps[:, c % MB, b * F:(b + 1) * F], xt_sb[:, c, b, :], t24[:],
                                          start=True, stop=True)
                mm.then_inc(y_mm.sem, 1)

            def hop(t, first, together):
                second = first >= K
                hi, lo = (z_hi, z_lo) if second else (y_hi, y_lo)
                th = t0 if second else t13
                prev = first - HB
                if isinstance(t, int) and t == 0 and FIRST <= first < FIRST + HB:
                    prev = HB - 1
                if prev >= K:
                    wait(pe, x1_done, t, prev - K)
                elif prev >= 0:
                    wait(pe, z_lo_done, t, prev)
                elif not (isinstance(t, int) and t == 0):
                    wait(pe, x1_done, t - 1, prev + K)
                for k in range(K):
                    if first % K == 0:
                        wait(pe, z_lo_done if second else y_lo_done, t, k)
                    if isinstance(t, int) and first == 0:
                        pe.wait_ge(a_hi_done, k + 1)
                        pe.wait_ge(a_lo_done, k + 1)
                    for slot in range(first, first + together):
                        c = slot % K
                        dst = hop_bank(t, slot)
                        for n, (sta, mov) in enumerate(((a_hi, hi), (a_hi, lo), (a_lo, hi))):
                            last = k == K - 1 and n == 2
                            if last:
                                for b in range(PAIR):
                                    nc.tensor.matmul(dst[:, b * F:(b + 1) * F], xt_sb[:, c, b, :], th[:],
                                                     start=False, stop=False)
                                if second:
                                    nc.tensor.matmul(dst.rearrange("p (b f) -> p b f", b=PAIR), ones[:],
                                                     bias_r[:].unsqueeze(1).broadcast_to([P, PAIR, F]), start=False, stop=False)
                            mm = nc.tensor.matmul(dst, sta[:, k, c * P:(c + 1) * P], mov[:, k, :],
                                                  start=(k == 0 and n == 0), stop=last)
                        if k == K - 1:
                            mm.then_inc(hop_mm.sem, 1)

            def pv(t, s, old=True):
                b, k = divmod(s, K)
                wait(pe, exp_done[1] if on_pool(s) else p_done, t, nth(s))
                if s == K:
                    wait(pe, elu_done, t, 0)
                if s == 0 and old:
                    wait(pe, elu_done, t - 1, 1)
                for i in range(K):
                    bank, at = divmod(i, PV_PER_BANK)
                    mm = nc.tensor.matmul(pv_ps[:, bank, at * PVW:(at + 1) * PVW],
                                          ring[:, s % RING, i * P:(i + 1) * P], haug[:, b, k, 0:PVW],
                                          start=(k == 0 and at == 0), stop=(k == K - 1), skip_group_check=True)
                mm.then_inc(pv_mm.sem, 1)

            def one_pass(t, layer0, new, old):
                u, o = t - 1, t - 2
                plan = BESIDE_LAYER0 if layer0 else ALONE
                if layer0:
                    for c in range(K):
                        project_y(t, c)
                if old:
                    pv(o, 8)
                    pv(o, 9)
                if new:
                    pe.wait_ge(w_done, 1)
                    for c in range(K):
                        transpose_x(t, c, layer0)
                if old:
                    pv(o, 10)
                if new:
                    for i in range(K // 2):
                        project_h(t, i)
                for slot in range(SLOTS):
                    if new and slot == H1_SLOT:
                        for i in range(K // 2, K):
                            project_h(t, i)
                    if layer0 and not new and slot == 0:
                        hop(t, 0, FIRST)
                    elif layer0 and (new or slot >= FIRST):
                        hop(t, slot, 1)
                    if layer0 and not new and slot == K:
                        w_a()
                    if old:
                        for s in OLD_PV_IN.get(slot, ()):
                            pv(o, s)
                    if new:
                        for s in plan["products"].get(slot, ()):
                            pv(u, s, old)

            passes(pe, one_pass)

        @block.vector
        def _(dve):
            v = nc.vector
            chain = [0]

            def link(ins):
                chain[0] += 1
                ins.then_inc(dve_setup, 1)
                dve.wait_ge(dve_setup, chain[0])

            dve.wait_ge(theta_in, 16)
            th = xres[:, 0]
            link(v.tensor_tensor(t24[:], th[:, 2, :], th[:, 4, :], ALU.add))
            v.tensor_tensor(t0[:], th[:, 0, :], t24[:], ALU.subtract).then_inc(theta_done, 1)
            v.tensor_tensor(t13[:], th[:, 1, :], th[:, 3, :], ALU.add).then_inc(theta_done, 1)
            dve.wait_ge(theta_done, 2)
            v.tensor_scalar(t24[:], t24[:], 2.0, None, ALU.mult).then_inc(theta_done, 1)

            def constants():
                dve.wait_ge(consts_in, 16 * 7)
                link(v.memset(haug[:, :, :, 0:1], 1.0))
                link(v.memset(xres[:, 1, 3, :], 1.0))
                link(v.tensor_copy(ones[:], xres[:, 1, 3, :]))
                link(v.memset(xres[:, 1, 4, :], 0.0))
                link(v.tensor_copy(bias_r[:, 0:F], xres[:, 1, 4, :]))
                two = slice(0, 2)
                link(v.tensor_copy(bias_r[two, 0:F], xres[two, 1, 2, :]))
                link(v.tensor_tensor(xres[two, 1, 3, :], xres[two, 1, 2, :], bias_r[two, 0:F].bitcast(F32), ALU.subtract))
                link(v.tensor_scalar(xres[two, 1, 4, :], bias_r[two, 0:F].bitcast(F32), ident[two, 0:1], None, ALU.mult))
                link(v.scalar_tensor_tensor(bias_r[two, 0:F], xres[two, 1, 3, :], ident[two, 1:2],
                                            xres[two, 1, 4, :], ALU.mult, ALU.add))

            def split_a_lo(k):
                dve.wait_ge(a_hi_done, k + 1)
                v.tensor_tensor(a_lo[:, k, :], ring[:, k, :], a_hi[:, k, :].bitcast(F32), ALU.subtract).then_inc(a_lo_done, 1)

            def neg_of(k):
                dve.wait_ge(a_lo_done, k + 1)
                link(v.tensor_scalar(neg[:, k, :], ring[:, k, :], 0.0, MASKED, ALU.is_le, ALU.mult))
                diag = ring[:, k, k * P:(k + 1) * P]
                link(v.tensor_tensor(diag, diag, ident[:], ALU.add))
                v.tensor_scalar(neg[:, k, k * P:(k + 1) * P], diag, 0.0, MASKED, ALU.is_le, ALU.mult).then_inc(neg_done, 1)

            def mask_of(k):
                to, ops = (neg_t, (MASKED, ALU.is_le, ALU.mult)) if on_pool(k) else (mask_t, (None, ALU.is_gt))
                dve.wait_ge(at_in[k], 16)
                link(v.tensor_scalar(to[:, nth(k), :], ring[:, k, :], 0.0, *ops))
                diag = ring[:, k, k * P:(k + 1) * P]
                link(v.tensor_tensor(diag, diag, ident[:], ALU.add))
                v.tensor_scalar(to[:, nth(k), k * P:(k + 1) * P], diag, 0.0, *ops).then_inc(mask_done, 1)

            def sub_y_lo(t, c):
                wait(dve, y_hi_done, t, c)
                v.tensor_tensor(y_lo[:, c, :], misc_ps[:, c % MB, 0:PAIR * F], y_hi[:, c, :].bitcast(F32),
                                ALU.subtract).then_inc(y_lo_done.sem, 1)

            def sub_z_lo(t, c):
                wait(dve, z_hi_done, t, c)
                v.tensor_tensor(z_lo[:, c, :], hop_bank(t, c), z_hi[:, c, :].bitcast(F32),
                                ALU.subtract).then_inc(z_lo_done.sem, 1)

            def residual0(t, c):
                if c == 0:
                    wait(dve, x_in, t, 0)
                wait(dve, hop_mm, t, K + c)
                v.scalar_tensor_tensor(xn[:, :, c, :], hop_ps[:, c % HB, 0:PAIR * F].rearrange("p (b f) -> p b f", b=PAIR),
                                       0.0, xn[:, :, c, :], ALU.max, ALU.add).then_inc(x1_done.sem, 1)
                wait(dve, x1_done, t, c)
                for b in range(PAIR):
                    last = v.bn_stats(stats1[:, b, :], xn[:, b, c, :])
                last.then_inc(bn1_done.sem, 1)
                wait(dve, bn1_done, t, c, theta_done)
                for b in range(PAIR):
                    last = v.bn_aggr(mv1[:, c, b, :], stats1[:, b, :])
                last.then_inc(mv1_done.sem, 1)

            def d_columns(t, b):
                wait(dve, h_ev, t, (b + 1) * K // 2 - 1)
                v.tensor_copy(d_col[:, b, :], haug[:, b, :, F + 2])
                v.tensor_scalar(d02[:, b, :], haug[:, b, :, F + 2], ALPHA, None, ALU.mult).then_inc(d_ready.sem, 1)

            def masked_max(t, b, k):
                if k == 0:
                    wait(dve, d_in[b], t, 0, theta_done)
                v.tensor_tensor_reduce(rows_ab[:, b, 1, :].rearrange("p (k q) -> p k q", k=K),
                                       neg[:, k, :].rearrange("p (k q) -> p k q", k=K),
                                       ring[:, D_TILE[b], :].rearrange("p (q k) -> p k q", k=K),
                                       1.0, 4 * MASKED, ALU.add, ALU.max, dmax[:, k:k + 1]).then_inc(max_done.sem, 1)
                wait(dve, max_done, t, b * K + k, theta_done)

            def ab_columns(t, b):
                s = haug[:, b, :, F + 1]
                v.tensor_tensor(dmax[:], s, dmax[:], ALU.add).then_inc(logit_done.sem, 1)
                wait(dve, logit_done, t, b)
                v.scalar_tensor_tensor(dmax[:], dmax[:], ALPHA, dmax[:], ALU.mult, ALU.max).then_inc(m_done.sem, 1)
                wait(dve, m_done, t, b)
                v.tensor_tensor(ab_col[:, b, 0, :], s, dmax[:], ALU.subtract)
                v.scalar_tensor_tensor(ab_col[:, b, 1, :], s, ALPHA, dmax[:], ALU.mult, ALU.subtract).then_inc(ab_ready.sem, 1)

            def exponent(t, s):
                b, k = divmod(s, K)
                if k == 0:
                    wait(dve, a_row_in[b], t, 0)
                wait(dve, t2_done, t, s)
                tile = ring[:, s % RING, :].rearrange("p (k q) -> p k q", k=K)
                v.scalar_tensor_tensor(tile, rows_ab[:, b, 0].rearrange("p (q k) -> p k q", k=K),
                                       haug[:, b, k, F + 2:F + 3], tile, ALU.add, ALU.max).then_inc(z_done.sem, 1)

            def mask_p(t, s):
                if not on_pool(s):
                    wait(dve, exp_done[0], t, nth(s))
                    v.tensor_tensor(ring[:, s % RING, :], ring[:, s % RING, :], mask_t[:, nth(s % K), :],
                                    ALU.min).then_inc(p_done.sem, 1)

            def row_sums(t, b):
                wait(dve, pv_mm, t, (b + 1) * K - 1)
                for bank in range(PV_BANKS):
                    lo, hi = bank * PV_PER_BANK, min(K, (bank + 1) * PV_PER_BANK)
                    last = v.reciprocal(rsum[:, b, lo:hi], pv_ps[:, bank, 0:(hi - lo - 1) * PVW + 1:PVW])
                last.then_inc(rsum_done.sem, 1)

            def residual1(t, b):
                wait(dve, elu_done, t, b)
                wait(dve, xres_in[b], t, 0)
                x1, relu, e = xres[:, b].rearrange("p k f -> p (k f)"), rows_ab[:, b, 0, :], rows_ab[:, b, 1, :]
                v.scalar_tensor_tensor(e, e, 1.0, x1, ALU.min, ALU.add).then_inc(w_sum.sem, 1)
                wait(dve, w_sum, t, b)
                v.scalar_tensor_tensor(relu, relu, -1.0, e, ALU.add, ALU.add).then_inc(y_done.sem, 1)

            def moments1(t, b):
                wait(dve, y_done, t, b)
                for k in range(K):
                    last = v.bn_stats(stats2[:, k, :], rows_ab[:, b, 0, k * F:(k + 1) * F])
                last.then_inc(bn2_done.sem, 1)
                wait(dve, bn2_done, t, b, theta_done)
                for k in range(K):
                    last = v.bn_aggr(mv2[:, b, k, :], stats2[:, k, :])
                last.then_inc(mv2_done.sem, 1)

            def make(u, plan, slot):
                for s in plan["steps"].get(slot, ()):
                    exponent(u, s)
                    if s and s != K:
                        mask_p(u, s - 1)

            def one_pass(t, layer0, new, old):
                u, o = t - 1, t - 2
                plan = BESIDE_LAYER0 if layer0 else ALONE
                if layer0:
                    for c in range(K):
                        sub_y_lo(t, c)
                    if not new:
                        for k in range(K):
                            split_a_lo(k)
                if old:
                    exponent(o, 10)
                    exponent(o, 11)
                    mask_p(o, 10)
                    residual1(o, 0)
                    exponent(o, 12)
                    mask_p(o, 11)
                    exponent(o, 13)
                    mask_p(o, 12)
                if new:
                    d_columns(u, 0)
                for slot in range(SLOTS):
                    if layer0 and slot < K:
                        sub_z_lo(t, slot)
                    if layer0 and not new:
                        if slot == 0:
                            constants()
                        (neg_of if slot < K else mask_of)(slot % K)
                    if old:
                        if slot < 2:
                            exponent(o, 14 + slot)
                        if slot < 3:
                            mask_p(o, 13 + slot)
                        if slot == 0:
                            moments1(o, 0)
                        if slot == OLD_SUMS_SLOT:
                            row_sums(o, 1)
                        if slot == plan["old_moments"]:
                            moments1(o, 1)
                    if new:
                        if slot == H1_SLOT + layer0:
                            d_columns(u, 1)
                        if slot in plan["maxes"]:
                            b, blocks = plan["maxes"][slot]
                            for k in blocks:
                                masked_max(u, b, k)
                            if blocks[-1] == K - 1:
                                ab_columns(u, b)
                        if slot == plan["sums"]:
                            row_sums(u, 0)
                        make(u, plan, slot)
                    if old and slot == plan["old_out"]:
                        residual1(o, 1)
                    if layer0 and slot >= K:
                        residual0(t, slot - K)
                    if new and K - 1 in plan["steps"].get(slot, ()):
                        mask_p(u, K - 1)

            passes(dve, one_pass)


def kernel(**inputs):
    import numpy as np
    import concourse.bacc as bacc
    from concourse.bass_utils import run_bass_kernel_spmd

    x, adj = np.asarray(inputs["x"]), np.asarray(inputs["adj"])
    theta, w = np.asarray(inputs["L0_gnn_Theta1"]), np.asarray(inputs["L1_gnn_W"])
    blocks = theta.shape[0] // F
    by_block = lambda a: a.reshape(P, K, P, K).transpose(0, 1, 3, 2).reshape(P, K, N)
    laid = {
        "x": x.reshape(GROUPS, PAIR, P, K, F).transpose(0, 2, 1, 3, 4),
        "xt": x.reshape(GROUPS, PAIR, P, K, F).transpose(0, 4, 3, 1, 2),
        "adj": by_block(adj),
        "adjt": by_block(adj.T),
        "theta": theta.reshape(blocks, F, F).transpose(1, 0, 2),
        "bias": np.asarray(inputs["L0_gnn_bias"]).reshape(1, F),
        "w": w,
        "wt": w.T,
        "a_src": np.asarray(inputs["L1_gnn_a_src"]),
        "a_dst": np.asarray(inputs["L1_gnn_a_dst"]),
        "ident_in": np.eye(P, dtype=np.float32),
    }
    laid = {name: np.ascontiguousarray(a) for name, a in laid.items()}
    nc = bacc.Bacc("TRN2", target_bir_lowering=False, num_devices=1)
    aps = {name: nc.dram_tensor(f"in_{name}", a.shape, mybir.dt.from_np(a.dtype), kind="ExternalInput").ap()
           for name, a in laid.items()}
    out = nc.dram_tensor("out_0", [GROUPS, P, PAIR, K, F], F32, kind="ExternalOutput").ap()
    chebyshev_then_attention(nc, out=out, **aps)
    r = run_bass_kernel_spmd(nc, [{f"in_{name}": a for name, a in laid.items()}], core_ids=[0])
    got = np.asarray(r.results[0]["out_0"])
    return got.reshape(GROUPS, P, PAIR, K, F).transpose(0, 2, 1, 3, 4).reshape(B, N, F)
```

```python
from contextlib import ExitStack, contextmanager

import concourse.bass as bass
from concourse import mybir

F32, F32R, BF16, U8 = mybir.dt.float32, mybir.dt.float32r, mybir.dt.bfloat16, mybir.dt.uint8
ALU = mybir.AluOpType
ACT = mybir.ActivationFunctionType

P = 128
B, N, F = 8, 1024, 128
K = N // P
PAIR = 2
GROUPS = B // PAIR
SLOTS = 2 * K
STEPS = PAIR * K
RING = 8
HB, MB = 2, 3
FIRST = HB + 3
BANK = 512
HW = F + 3
PVW = F + 1
PV_PER_BANK = BANK // PVW
PV_BANKS = -(-K // PV_PER_BANK)
ALPHA, EPS, MASKED = 0.2, 1e-5, -1e30
XT_TILE, D_TILE = 0, (2, 7)

BESIDE_LAYER0 = dict(
    maxes={0: (0, (0,)), 1: (0, (1, 2, 3)), 2: (0, (4, 5, 6, 7)),
           8: (1, (0, 1)), 9: (1, (2, 3)), 10: (1, (4, 5)), 11: (1, (6, 7))},
    steps={5: (0,), 6: (1,), 8: (2,), 9: (3,), 10: (4, 5), 11: (6,), 12: (7,), 13: (8,), 14: (9,), 15: (10,)},
    products={8: (0,), 9: (1,), 10: (2,), 11: (3, 4), 12: (5,), 13: (6, 7)},
    sums=14, old_out=(4, 5), old_moments=6, ahead=1)
ALONE = dict(
    maxes={2: (0, (0, 1, 2, 3)), 3: (0, (4, 5, 6, 7)), 5: (1, (0, 1)), 6: (1, (2, 3)), 7: (1, (4, 5)), 8: (1, (6, 7))},
    steps={6: (0,), 7: (1,), 8: (2,), 9: (3,), 10: (4,), 11: (5,), 12: (6,), 13: (7,), 14: (8, 9), 15: (10,)},
    products={7: (0,), 8: (1,), 9: (2,), 10: (3,), 11: (4,), 12: (5,), 13: (6,), 14: (7,)},
    sums=15, old_out=(4, 4), old_moments=5, ahead=2)
OLD_PV_IN = {0: (11, 12), 1: (13, 14), 2: (15,)}
POOL_BLOCKS = (1, 3, 5)
MADE, MULTIPLIED = 11, 8
H1_SLOT = 3
OLD_SUMS_SLOT = 3


def blocks_of(half):
    return slice(half * K // 2, (half + 1) * K // 2)


def on_pool(s):
    return s % K in POOL_BLOCKS


def nth(s):
    return sum(on_pool(e) == on_pool(s) for e in range(s))


class Signal:

    def __init__(self, sem, per, first, unit=1):
        self.sem, self.per, self.first, self.unit = sem, per, first, unit

    def level(self, t, i):
        return (t - self.first) * (self.per * self.unit) + (i + 1) * self.unit


@contextmanager
def in_register(eng, level):
    register = level
    if not isinstance(level, int):
        register = eng.alloc_register()
        eng.reg_mov(register, level)
    yield register
    if not isinstance(level, int):
        eng.free_register(register)


def chebyshev_then_attention(nc, x, xt, adj, adjt, theta, bias, w, wt, a_src, a_dst, ident_in, out):
    with ExitStack() as ctx:
        def sb(name, shape, dt=F32):
            return ctx.enter_context(nc.sbuf_tensor(name, shape, dt))

        def sem(name):
            return ctx.enter_context(nc.semaphore(name))

        a_hi = sb("a_hi", [P, K, N], F32R)
        a_lo = sb("a_lo", [P, K, N], F32R)
        neg = sb("neg", [P, K, N], BF16)
        mask_t = sb("mask_t", [P, K - len(POOL_BLOCKS), N], U8)
        neg_t = sb("neg_t", [P, len(POOL_BLOCKS), N], BF16)
        y_hi = sb("y_hi", [P, K, PAIR * F], F32R)
        y_lo = sb("y_lo", [P, K, PAIR * F], F32R)
        z_hi = sb("z_hi", [P, K, PAIR * F], F32R)
        z_lo = sb("z_lo", [P, K, PAIR * F], F32R)
        xt_sb = sb("xt_sb", [P, K, PAIR, P])
        xn = sb("xn", [P, PAIR, K, F])
        xres = sb("xres", [P, PAIR, K, F])
        haug = sb("haug", [P, PAIR, K, HW])
        rows_ab = sb("rows_ab", [P, PAIR, 2, N])
        ring = sb("ring", [P, RING, N])
        ident = sb("ident", [P, P])
        t24 = sb("t24", [P, F])
        t13 = sb("t13", [P, F])
        t0 = sb("t0", [P, F])
        w_aug = sb("w_aug", [P, F + 2])
        ones = sb("ones", [P, P], F32R)
        bias_r = sb("bias_r", [P, F], F32R)
        minus_half = sb("minus_half", [P, K])
        stats1 = sb("stats1", [P, PAIR, 6])
        mv1 = sb("mv1", [P, K, PAIR, 2])
        rstd1 = sb("rstd1", [P, K, PAIR])
        nmr1 = sb("nmr1", [P, K, PAIR])
        stats2 = sb("stats2", [P, K, 6])
        mv2 = sb("mv2", [P, PAIR, K, 2])
        rstd2 = sb("rstd2", [P, PAIR, K])
        nmr2 = sb("nmr2", [P, PAIR, K])
        d_col = sb("d_col", [P, PAIR, K])
        d02 = sb("d02", [P, PAIR, K])
        dmax = sb("dmax", [P, K])
        ab_col = sb("ab_col", [P, PAIR, 2, K])
        rsum = sb("rsum", [P, PAIR, K])
        hop_ps = ctx.enter_context(nc.psum_tensor("hop_ps", [P, HB, BANK], F32))
        misc_ps = ctx.enter_context(nc.psum_tensor("misc_ps", [P, MB, BANK], F32))
        pv_ps = ctx.enter_context(nc.psum_tensor("pv_ps", [P, PV_BANKS, BANK], F32))
        d_row = nc.dram_tensor("d_row", [PAIR, P, K], F32, kind="Internal").ap()
        ab_row = nc.dram_tensor("ab_row", [PAIR, 2, P, K], F32, kind="Internal").ap()

        consts_in, theta_in = sem("consts_in"), sem("theta_in")
        a_in = [sem(f"a_in{k}") for k in range(K)]
        at_in = [sem(f"at_in{k}") for k in range(K)]
        a_hi_done, a_lo_done, neg_done, mask_done = sem("a_hi_done"), sem("a_lo_done"), sem("neg_done"), sem("mask_done")
        theta_done, wa_mm, w_done, half_done, dve_setup = (
            sem("theta_done"), sem("wa_mm"), sem("w_done"), sem("half_done"), sem("dve_setup"))
        xt_in = [Signal(sem(f"xt_in{c}"), 1, 0, 16) for c in range(K)]
        x_in = Signal(sem("x_in"), 1, 0, 16)
        y_mm, y_hi_done, y_lo_done = (Signal(sem(s), K, 0) for s in ("y_mm", "y_hi_done", "y_lo_done"))
        hop_mm = Signal(sem("hop_mm"), SLOTS, 0)
        z_hi_done, z_lo_done = (Signal(sem(s), K, 0) for s in ("z_hi_done", "z_lo_done"))
        x1_done, bn1_done, mv1_done, eps1_done, rstd1_done, nmr1_done, xn_done = (
            Signal(sem(s), K, 0) for s in ("x1_done", "bn1_done", "mv1_done", "eps1_done", "rstd1_done", "nmr1_done", "xn_done"))
        tr_mm, xt_ev, h_mm, h_ev = (Signal(sem(s), K, 0) for s in ("tr_mm", "xt_ev", "h_mm", "h_ev"))
        xres_in = [Signal(sem(f"xres_in{b}"), 1, 0, 16) for b in range(PAIR)]
        d_ready, ab_ready = (Signal(sem(s), PAIR, 0) for s in ("d_ready", "ab_ready"))
        d_out, ab_out = (Signal(sem(s), PAIR, 0, 16) for s in ("d_out", "ab_out"))
        d_in = [Signal(sem(f"d_in{b}"), 1, 0, 16) for b in range(PAIR)]
        a_row_in = [Signal(sem(f"a_row_in{b}"), 1, 0, 16) for b in range(PAIR)]
        b_row_in = [Signal(sem(f"b_row_in{b}"), 1, 0, 16) for b in range(PAIR)]
        max_done, logit_done, m_done = Signal(sem("max_done"), STEPS, 0), Signal(sem("logit_done"), PAIR, 0), Signal(sem("m_done"), PAIR, 0)
        t2_done, z_done, pv_mm = (
            Signal(sem(s), STEPS, 0) for s in ("t2_done", "z_done", "pv_mm"))
        on_dve = STEPS - PAIR * len(POOL_BLOCKS)
        exp_done = (Signal(sem("exp_done"), on_dve, 0), Signal(sem("masked_exp_done"), STEPS - on_dve, 0))
        zm_done, p_done = Signal(sem("zm_done"), STEPS - on_dve, 0), Signal(sem("p_done"), on_dve, 0)
        rsum_done = Signal(sem("rsum_done"), PAIR, 0)
        elu_done, w_sum, y_done, bn2_done, mv2_done, eps2_done, rstd2_done, nmr2_done, out_done = (
            Signal(sem(s), PAIR * 2, 0) for s in
            ("elu_done", "w_sum", "y_done", "bn2_done", "mv2_done", "eps2_done", "rstd2_done", "nmr2_done", "out_done"))
        out_stored = [Signal(sem(f"out_stored{b}"), 2, 0, 16) for b in range(PAIR)]

        def passes(eng, one_pass):
            one_pass(0, True, False, False)
            one_pass(1, True, True, False)
            with eng.Fori(2, GROUPS) as t:
                one_pass(t, True, True, True)
            one_pass(GROUPS, False, True, True)
            one_pass(GROUPS + 1, False, False, True)

        def misc_free(eng, t, pos, layer0):
            prev = pos - MB
            if prev >= 2 * K:
                eng.wait_ge(h_ev.sem, h_ev.level(t - 1, prev - 2 * K))
            elif prev >= K:
                eng.wait_ge(xt_ev.sem, xt_ev.level(t - 1, prev - K))
            elif prev >= 0 and layer0:
                eng.wait_ge(y_lo_done.sem, y_lo_done.level(t, prev))

        def hop_bank(t, slot):
            if isinstance(t, int) and t == 0 and HB <= slot < FIRST:
                return pv_ps[:, slot - HB, 0:PAIR * F]
            return hop_ps[:, slot % HB, 0:PAIR * F]

        block = ctx.enter_context(nc.Block())

        @block.sync
        def _(sp):
            for c in range(1, K, 2):
                sp.dma_start(xt_sb[:, c], xt[0][:, c]).then_inc(xt_in[c].sem, 16)
            for k in range(K):
                sp.dma_start(ring[:, k, :], adj[:, k, :]).then_inc(a_in[k], 16)
            for dst, src in ((ident[:], ident_in), (w_aug[:, 0:F], w)):
                sp.dma_start(dst, src).then_inc(consts_in, 16)
            sp.dma_start(xres[:, 1, 0, :], wt).then_inc(consts_in, 16)
            sp.dma_start(xres[:, 1, 1, 0:1], a_src).then_inc(consts_in, 16)
            sp.dma_start(xres[:, 1, 1, 1:2], a_dst).then_inc(consts_in, 16)
            sp.dma_start(xres[0:1, 1, 2, :], bias).then_inc(consts_in, 16)
            sp.dma_start(xres[1:2, 1, 2, :], bias).then_inc(consts_in, 16)
            sp.dma_start(xn[:], x[0]).then_inc(x_in.sem, 16)
            for k in range(K):
                sp.wait_ge(a_hi_done, k + 1)
                sp.wait_ge(a_lo_done, k + 1)
                sp.wait_ge(neg_done, k + 1)
                sp.dma_start(ring[:, k, :], adjt[:, k, :]).then_inc(at_in[k], 16)

            def d_to_dram(u, b):
                sp.wait_ge(d_ready.sem, d_ready.level(u, b))
                sp.dma_start(d_row[b], d_col[:, b, :]).then_inc(d_out.sem, 16)

            def d_to_all(u, b):
                sp.wait_ge(d_out.sem, d_out.level(u, b))
                sp.dma_start(ring[:, D_TILE[b], :],
                             d_row[b].rearrange("(o p) k -> o (p k)", o=1).broadcast_to([P, N])).then_inc(d_in[b].sem, 16)

            def ab_to_dram(u, b):
                sp.wait_ge(ab_ready.sem, ab_ready.level(u, b))
                sp.dma_start(ab_row[b].rearrange("a p k -> p a k"), ab_col[:, b]).then_inc(ab_out.sem, 16)

            def ab_to_all(u, b, old):
                if old:
                    with in_register(sp, out_stored[b].level(u - 1, 1)) as level:
                        sp.wait_ge(theta_done, 1)
                        sp.wait_ge(out_stored[b].sem, level)
                sp.wait_ge(ab_out.sem, ab_out.level(u, b))
                for a, signal in ((1, b_row_in), (0, a_row_in)):
                    sp.dma_start(rows_ab[:, b, a], ab_row[b, a].rearrange("(o p) k -> o (p k)", o=1).broadcast_to([P, N])
                                 ).then_inc(signal[b].sem, 16)

            def x_to_residual(u, b, old):
                if old:
                    with in_register(sp, y_done.level(u - 1, 2 * b + 1)) as level:
                        sp.wait_ge(theta_done, 1)
                        sp.wait_ge(y_done.sem, level)
                sp.wait_ge(xn_done.sem, xn_done.level(u, K - 1))
                sp.dma_start(xres[:, b], xn[:, b]).then_inc(xres_in[b].sem, 16)

            def one_pass(t, layer0, new, old):
                if not new:
                    return
                u = t - 1
                d_to_dram(u, 0)
                d_to_all(u, 0)
                x_to_residual(u, 0, old)
                if not layer0:
                    d_to_dram(u, 1)
                    d_to_all(u, 1)
                ab_to_dram(u, 0)
                ab_to_all(u, 0, old)
                if layer0:
                    d_to_dram(u, 1)
                    d_to_all(u, 1)
                x_to_residual(u, 1, old)
                if layer0:
                    for b in range(PAIR):
                        with in_register(sp, xres_in[b].level(u, 0)) as level:
                            sp.wait_ge(theta_done, 1)
                            sp.wait_ge(xres_in[b].sem, level)
                    sp.wait_ge(tr_mm.sem, tr_mm.level(u, K - 1))
                    sp.dma_start(xn[:], x[t]).then_inc(x_in.sem, 16)
                ab_to_dram(u, 1)
                ab_to_all(u, 1, old)

            passes(sp, one_pass)
            for b in range(PAIR):
                sp.wait_ge(out_stored[b].sem, out_stored[b].level(GROUPS - 1, 1))

        @block.gpsimd
        def _(pool):
            nc.gpsimd.memset(minus_half[:], -0.5).then_inc(half_done, 1)
            pool.wait_ge(half_done, 1)

            def rstd1_of(t, c):
                with in_register(pool, mv1_done.level(t, c)) as level:
                    pool.wait_ge(half_done, 1)
                    pool.wait_ge(mv1_done.sem, level)
                nc.gpsimd.tensor_scalar(rstd1[:, c, :], mv1[:, c, :, 1], EPS, 1.0, ALU.add, ALU.mult)
                nc.gpsimd.tensor_scalar(nmr1[:, c, :], mv1[:, c, :, 0], -1.0, 0.0, ALU.mult, ALU.add).then_inc(eps1_done.sem, 1)
                pool.wait_ge(eps1_done.sem, eps1_done.level(t, c))
                nc.gpsimd.tensor_tensor(rstd1[:, c, :], rstd1[:, c, :], minus_half[:, 0:PAIR], ALU.pow).then_inc(rstd1_done.sem, 1)
                pool.wait_ge(rstd1_done.sem, rstd1_done.level(t, c))
                nc.gpsimd.tensor_tensor(nmr1[:, c, :], nmr1[:, c, :], rstd1[:, c, :], ALU.mult).then_inc(nmr1_done.sem, 1)

            def norm2_of(t, b):
                for half in (0, 1):
                    at, i = blocks_of(half), 2 * b + half
                    with in_register(pool, mv2_done.level(t, i)) as level:
                        pool.wait_ge(half_done, 1)
                        pool.wait_ge(mv2_done.sem, level)
                    nc.gpsimd.tensor_scalar(rstd2[:, b, at], mv2[:, b, at, 1], EPS, 1.0, ALU.add, ALU.mult)
                    nc.gpsimd.tensor_scalar(nmr2[:, b, at], mv2[:, b, at, 0], -1.0, 0.0, ALU.mult, ALU.add).then_inc(eps2_done.sem, 1)
                    pool.wait_ge(eps2_done.sem, eps2_done.level(t, i))
                    nc.gpsimd.tensor_tensor(rstd2[:, b, at], rstd2[:, b, at], minus_half[:, at], ALU.pow).then_inc(rstd2_done.sem, 1)
                    pool.wait_ge(rstd2_done.sem, rstd2_done.level(t, i))
                    nc.gpsimd.tensor_tensor(nmr2[:, b, at], nmr2[:, b, at], rstd2[:, b, at], ALU.mult).then_inc(nmr2_done.sem, 1)

            def store(t, b):
                for half in (0, 1):
                    with in_register(pool, out_done.level(t, 2 * b + half)) as level:
                        pool.wait_ge(half_done, 1)
                        pool.wait_ge(out_done.sem, level)
                    pool.dma_start(out[t][:, b, blocks_of(half)],
                                   rows_ab[:, b, 0, :].rearrange("p (k f) -> p k f", k=K)[:, blocks_of(half)]
                                   ).then_inc(out_stored[b].sem, 16)

            def mask_z(t, s):
                if on_pool(s):
                    pool.wait_ge(z_done.sem, z_done.level(t, s))
                    nc.gpsimd.tensor_tensor(ring[:, s % RING, :], ring[:, s % RING, :], neg_t[:, nth(s % K), :],
                                            ALU.add).then_inc(zm_done.sem, 1)

            def one_pass(t, layer0, new, old):
                u, o = t - 1, t - 2
                plan = BESIDE_LAYER0 if layer0 else ALONE
                if old:
                    mask_z(o, 11)
                    mask_z(o, 13)
                    norm2_of(o, 0)
                    store(o, 0)
                for slot in range(SLOTS):
                    if old and slot == plan["old_moments"] + 1:
                        norm2_of(o, 1)
                    if new:
                        for s in plan["steps"].get(slot, ()):
                            mask_z(u, s)
                    if old and slot == plan["old_moments"] + 2:
                        store(o, 1)
                    if layer0 and slot >= K:
                        rstd1_of(t, slot - K)

            passes(pool, one_pass)

        @block.scalar
        def _(act):
            act.dma_start(xres[:, 0, 0:5, :], theta).then_inc(theta_in, 16)
            for c in range(0, K, 2):
                act.dma_start(xt_sb[:, c], xt[0][:, c]).then_inc(xt_in[c].sem, 16)

            def split_a_hi(k):
                act.wait_ge(a_in[k], 16)
                nc.scalar.copy(a_hi[:, k, :], ring[:, k, :]).then_inc(a_hi_done, 1)

            def copy_y_hi(t, c):
                act.wait_ge(y_mm.sem, y_mm.level(t, c))
                if not (isinstance(t, int) and t == 0):
                    act.wait_ge(hop_mm.sem, hop_mm.level(t - 1, K - 1))
                nc.scalar.copy(y_hi[:, c, :], misc_ps[:, c % MB, 0:PAIR * F]).then_inc(y_hi_done.sem, 1)

            def copy_z_hi(t, c):
                act.wait_ge(hop_mm.sem, hop_mm.level(t, c))
                if not (isinstance(t, int) and t == 0):
                    act.wait_ge(hop_mm.sem, hop_mm.level(t - 1, SLOTS - 1))
                nc.scalar.copy(z_hi[:, c, :], hop_bank(t, c)).then_inc(z_hi_done.sem, 1)

            def normalise0(t, c):
                act.wait_ge(nmr1_done.sem, nmr1_done.level(t, c))
                for b in range(PAIR):
                    last = nc.scalar.activation(xn[:, b, c, :], xn[:, b, c, :], ACT.Identity,
                                                bias=nmr1[:, c, b:b + 1], scale=rstd1[:, c, b:b + 1])
                last.then_inc(xn_done.sem, 1)

            def next_xt(t, c):
                act.wait_ge(hop_mm.sem, hop_mm.level(t, K + c))
                act.dma_start(xt_sb[:, c], xt[(t + 1) % GROUPS][:, c]).then_inc(xt_in[c].sem, 16)

            def second_branch(t, s, old=True):
                b, k = divmod(s, K)
                if k == 0:
                    act.wait_ge(b_row_in[b].sem, b_row_in[b].level(t, 0))
                if s == XT_TILE + 1:
                    act.wait_ge(h_mm.sem, h_mm.level(t, K - 1))
                elif s == D_TILE[1]:
                    act.wait_ge(max_done.sem, max_done.level(t, STEPS - 1))
                elif s >= RING:
                    act.wait_ge(pv_mm.sem, pv_mm.level(t, s - RING))
                elif s >= MULTIPLIED - RING and old:
                    act.wait_ge(pv_mm.sem, pv_mm.level(t - 1, s + STEPS - RING))
                nc.scalar.activation(ring[:, s % RING, :].rearrange("p (k q) -> p k q", k=K),
                                     rows_ab[:, b, 1].rearrange("p (q k) -> p k q", k=K),
                                     ACT.Identity, bias=d02[:, b, k:k + 1], scale=1.0).then_inc(t2_done.sem, 1)

            def exp(t, s):
                if on_pool(s):
                    act.wait_ge(zm_done.sem, zm_done.level(t, nth(s)))
                else:
                    act.wait_ge(z_done.sem, z_done.level(t, s))
                nc.scalar.activation(ring[:, s % RING, :], ring[:, s % RING, :], ACT.Exp).then_inc(exp_done[on_pool(s)].sem, 1)

            def elu_parts(t, b, half):
                act.wait_ge(rsum_done.sem, rsum_done.level(t, b))
                for i in range(half * K // 2, (half + 1) * K // 2):
                    src = pv_ps[:, i // PV_PER_BANK, (i % PV_PER_BANK) * PVW + 1:(i % PV_PER_BANK + 1) * PVW]
                    nc.scalar.activation(rows_ab[:, b, 0, i * F:(i + 1) * F], src, ACT.Relu, scale=rsum[:, b, i:i + 1])
                    last = nc.scalar.activation(rows_ab[:, b, 1, i * F:(i + 1) * F], src, ACT.Exp, scale=rsum[:, b, i:i + 1])
                last.then_inc(elu_done.sem, 1)

            def copy_xt(u, c):
                act.wait_ge(tr_mm.sem, tr_mm.level(u, c))
                nc.scalar.copy(ring[:, XT_TILE:XT_TILE + PAIR, c * P:(c + 1) * P],
                               misc_ps[:, (K + c) % MB, 0:PAIR * P].rearrange("p (b q) -> p b q", b=PAIR)).then_inc(xt_ev.sem, 1)

            def copy_h(u, i):
                b, half = divmod(i, K // 2)
                act.wait_ge(h_mm.sem, h_mm.level(u, i))
                nc.scalar.copy(haug[:, b, 2 * half:2 * half + 2, 1:HW],
                               misc_ps[:, (2 * K + i) % MB, :].rearrange("p (e n) -> p e n", e=2)[:, :, 0:F + 2]
                               ).then_inc(h_ev.sem, 1)

            def late(plan, slot, s):
                return on_pool(s) or plan is BESIDE_LAYER0 and slot < K

            def last_made(o):
                second_branch(o, MADE)
                exp(o, MADE - 1)
                second_branch(o, MADE + 1)

            def make(u, plan, slot, old):
                for s in plan["steps"].get(slot, ()):
                    if plan is BESIDE_LAYER0 and s == MADE - 1:
                        continue
                    if s == 0:
                        for first in range(plan["ahead"]):
                            second_branch(u, first, old)
                    ahead = s + plan["ahead"]
                    if ahead < K:
                        second_branch(u, ahead, old)
                    if not late(plan, slot, s):
                        exp(u, s)
                    if K <= ahead <= MADE:
                        second_branch(u, ahead, old)

            def normalise1(t, b):
                for k in range(K):
                    if k % (K // 2) == 0:
                        act.wait_ge(nmr2_done.sem, nmr2_done.level(t, 2 * b + k // (K // 2)))
                    y = rows_ab[:, b, 0, k * F:(k + 1) * F]
                    last = nc.scalar.activation(y, y, ACT.Identity, bias=nmr2[:, b, k:k + 1], scale=rstd2[:, b, k:k + 1])
                    if k % (K // 2) == K // 2 - 1:
                        last.then_inc(out_done.sem, 1)

            def one_pass(t, layer0, new, old):
                u, o = t - 1, t - 2
                plan = BESIDE_LAYER0 if layer0 else ALONE
                if new and not layer0:
                    if old:
                        last_made(o)
                    normalise0(u, K - 1)
                if layer0:
                    for c in range(K):
                        copy_y_hi(t, c)
                        if new and c == K // 2:
                            normalise0(u, K - 1)
                        if old and c == MB - 1:
                            last_made(o)
                    if not new:
                        for k in range(K):
                            split_a_hi(k)
                if old:
                    if not new:
                        second_branch(o, 12)
                    second_branch(o, 13)
                if new:
                    for c in range(K):
                        copy_xt(u, c)
                if old:
                    exp(o, 11)
                    second_branch(o, 14)
                    exp(o, 12)
                if new:
                    for i in range(K // 2):
                        copy_h(u, i)
                if old:
                    exp(o, 13)
                    second_branch(o, 15)
                for slot in range(SLOTS):
                    if new and slot == H1_SLOT:
                        for i in range(K // 2, K):
                            copy_h(u, i)
                    if layer0 and slot < K:
                        copy_z_hi(t, slot)
                    if slot == K and not new and layer0:
                        act.wait_ge(wa_mm, 1)
                        nc.scalar.copy(w_aug[:, F:F + 2], pv_ps[:, 0, 0:2]).then_inc(w_done, 1)
                    if new:
                        for s in plan["steps"].get(slot - 1, ()):
                            if late(plan, slot - 1, s):
                                exp(u, s)
                    if old:
                        if slot == 0:
                            exp(o, 14)
                        if slot == 1:
                            exp(o, 15)
                            normalise1(o, 0)
                        if slot in (OLD_SUMS_SLOT, OLD_SUMS_SLOT + 1):
                            elu_parts(o, 1, slot - OLD_SUMS_SLOT)
                        if slot == plan["old_moments"] + 1:
                            normalise1(o, 1)
                    if new:
                        if slot == plan["sums"]:
                            elu_parts(u, 0, 0)
                            elu_parts(u, 0, 1)
                        make(u, plan, slot, old)
                    if layer0 and slot > K:
                        next_xt(t, slot - K - 1)
                        normalise0(t, slot - K - 1)
                if layer0:
                    next_xt(t, K - 1)

            passes(act, one_pass)
            for c in range(K):
                act.wait_ge(xt_in[c].sem, xt_in[c].level(GROUPS, 0))

        @block.tensor
        def _(pe):
            def w_a():
                pe.wait_ge(consts_in, 16 * 7)
                nc.tensor.matmul(pv_ps[:, 0, 0:2], xres[:, 1, 0, :], xres[:, 1, 1, 0:2], start=True, stop=True).then_inc(wa_mm, 1)

            pe.wait_ge(theta_done, 3)

            def transpose_x(t, c, layer0):
                pe.wait_ge(xn_done.sem, xn_done.level(t - 1, c))
                misc_free(pe, t, K + c, layer0)
                for b in range(PAIR):
                    mm = nc.tensor.transpose(misc_ps[:, (K + c) % MB, b * P:(b + 1) * P], xn[:, b, c, :], ident[:])
                mm.then_inc(tr_mm.sem, 1)

            def project_h(t, i):
                b, half = divmod(i, K // 2)
                pe.wait_ge(xt_ev.sem, xt_ev.level(t - 1, 2 * half + 1))
                misc_free(pe, t, 2 * K + i, True)
                for e in range(2):
                    k = 2 * half + e
                    mm = nc.tensor.matmul(misc_ps[:, (2 * K + i) % MB, e * 256:e * 256 + F + 2],
                                          ring[:, XT_TILE + b, k * P:(k + 1) * P], w_aug[:], start=True, stop=True)
                mm.then_inc(h_mm.sem, 1)

            def project_y(t, c):
                pe.wait_ge(xt_in[c].sem, xt_in[c].level(t, 0))
                misc_free(pe, t, c, True)
                for b in range(PAIR):
                    mm = nc.tensor.matmul(misc_ps[:, c % MB, b * F:(b + 1) * F], xt_sb[:, c, b, :], t24[:],
                                          start=True, stop=True)
                mm.then_inc(y_mm.sem, 1)

            def hop(t, first, together):
                second = first >= K
                hi, lo = (z_hi, z_lo) if second else (y_hi, y_lo)
                th = t0 if second else t13
                prev = first - HB
                if isinstance(t, int) and t == 0 and FIRST <= first < FIRST + HB:
                    prev = HB - 1
                if prev >= K:
                    pe.wait_ge(x1_done.sem, x1_done.level(t, prev - K))
                elif prev >= 0:
                    pe.wait_ge(z_lo_done.sem, z_lo_done.level(t, prev))
                elif not (isinstance(t, int) and t == 0):
                    pe.wait_ge(x1_done.sem, x1_done.level(t - 1, prev + K))
                for k in range(K):
                    if first % K == 0:
                        halves_done = z_lo_done if second else y_lo_done
                        pe.wait_ge(halves_done.sem, halves_done.level(t, k))
                    if isinstance(t, int) and first == 0:
                        pe.wait_ge(a_hi_done, k + 1)
                        pe.wait_ge(a_lo_done, k + 1)
                    for slot in range(first, first + together):
                        c = slot % K
                        dst = hop_bank(t, slot)
                        for n, (sta, mov) in enumerate(((a_hi, hi), (a_hi, lo), (a_lo, hi))):
                            last = k == K - 1 and n == 2
                            if last:
                                for b in range(PAIR):
                                    nc.tensor.matmul(dst[:, b * F:(b + 1) * F], xt_sb[:, c, b, :], th[:],
                                                     start=False, stop=False)
                                if second:
                                    nc.tensor.matmul(dst.rearrange("p (b f) -> p b f", b=PAIR), ones[:],
                                                     bias_r[:].unsqueeze(1).broadcast_to([P, PAIR, F]), start=False, stop=False)
                            mm = nc.tensor.matmul(dst, sta[:, k, c * P:(c + 1) * P], mov[:, k, :],
                                                  start=(k == 0 and n == 0), stop=last)
                        if k == K - 1:
                            mm.then_inc(hop_mm.sem, 1)

            def pv(t, s, old=True):
                b, k = divmod(s, K)
                ready = exp_done[1] if on_pool(s) else p_done
                pe.wait_ge(ready.sem, ready.level(t, nth(s)))
                if s == K:
                    pe.wait_ge(elu_done.sem, elu_done.level(t, 1))
                if s == 0 and old:
                    pe.wait_ge(elu_done.sem, elu_done.level(t - 1, 3))
                for i in range(K):
                    bank, at = divmod(i, PV_PER_BANK)
                    mm = nc.tensor.matmul(pv_ps[:, bank, at * PVW:(at + 1) * PVW],
                                          ring[:, s % RING, i * P:(i + 1) * P], haug[:, b, k, 0:PVW],
                                          start=(k == 0 and at == 0), stop=(k == K - 1), skip_group_check=True)
                mm.then_inc(pv_mm.sem, 1)

            def one_pass(t, layer0, new, old):
                u, o = t - 1, t - 2
                plan = BESIDE_LAYER0 if layer0 else ALONE
                for c in range(K):
                    if layer0:
                        project_y(t, c)
                    if old and c in (MB - 1, 2 * MB - 1):
                        pv(o, 8 + c // MB)
                if new:
                    pe.wait_ge(w_done, 1)
                    for c in range(K):
                        transpose_x(t, c, layer0)
                if old:
                    pv(o, 10)
                if new:
                    for i in range(K // 2):
                        project_h(t, i)
                for slot in range(SLOTS):
                    if new and slot == H1_SLOT:
                        for i in range(K // 2, K):
                            project_h(t, i)
                    if layer0 and not new and slot == 0:
                        hop(t, 0, FIRST)
                    elif layer0 and (new or slot >= FIRST):
                        hop(t, slot, 1)
                    if layer0 and not new and slot == K:
                        w_a()
                    if old:
                        for s in OLD_PV_IN.get(slot, ()):
                            pv(o, s)
                    if new:
                        for s in plan["products"].get(slot, ()):
                            pv(u, s, old)

            passes(pe, one_pass)

        @block.vector
        def _(dve):
            v = nc.vector
            chain = [0]

            def link(ins):
                chain[0] += 1
                ins.then_inc(dve_setup, 1)
                dve.wait_ge(dve_setup, chain[0])

            dve.wait_ge(theta_in, 16)
            th = xres[:, 0]
            link(v.tensor_tensor(t24[:], th[:, 2, :], th[:, 4, :], ALU.add))
            v.tensor_tensor(t0[:], th[:, 0, :], t24[:], ALU.subtract).then_inc(theta_done, 1)
            v.tensor_tensor(t13[:], th[:, 1, :], th[:, 3, :], ALU.add).then_inc(theta_done, 1)
            dve.wait_ge(theta_done, 2)
            v.tensor_scalar(t24[:], t24[:], 2.0, None, ALU.mult).then_inc(theta_done, 1)

            def constants():
                dve.wait_ge(consts_in, 16 * 7)
                link(v.memset(haug[:, :, :, 0:1], 1.0))
                link(v.memset(xres[:, 1, 3, :], 1.0))
                link(v.tensor_copy(ones[:], xres[:, 1, 3, :]))
                link(v.memset(xres[:, 1, 4, :], 0.0))
                link(v.tensor_copy(bias_r[:, 0:F], xres[:, 1, 4, :]))
                two = slice(0, 2)
                link(v.tensor_copy(bias_r[two, 0:F], xres[two, 1, 2, :]))
                link(v.tensor_tensor(xres[two, 1, 3, :], xres[two, 1, 2, :], bias_r[two, 0:F].bitcast(F32), ALU.subtract))
                link(v.tensor_scalar(xres[two, 1, 4, :], bias_r[two, 0:F].bitcast(F32), ident[two, 0:1], None, ALU.mult))
                link(v.scalar_tensor_tensor(bias_r[two, 0:F], xres[two, 1, 3, :], ident[two, 1:2],
                                            xres[two, 1, 4, :], ALU.mult, ALU.add))

            def split_a_lo(k):
                dve.wait_ge(a_hi_done, k + 1)
                v.tensor_tensor(a_lo[:, k, :], ring[:, k, :], a_hi[:, k, :].bitcast(F32), ALU.subtract).then_inc(a_lo_done, 1)

            def neg_of(k):
                dve.wait_ge(a_lo_done, k + 1)
                link(v.tensor_scalar(neg[:, k, :], ring[:, k, :], 0.0, MASKED, ALU.is_le, ALU.mult))
                diag = ring[:, k, k * P:(k + 1) * P]
                link(v.tensor_tensor(diag, diag, ident[:], ALU.add))
                v.tensor_scalar(neg[:, k, k * P:(k + 1) * P], diag, 0.0, MASKED, ALU.is_le, ALU.mult).then_inc(neg_done, 1)

            def mask_of(k):
                to, ops = (neg_t, (MASKED, ALU.is_le, ALU.mult)) if on_pool(k) else (mask_t, (None, ALU.is_gt))
                dve.wait_ge(at_in[k], 16)
                link(v.tensor_scalar(to[:, nth(k), :], ring[:, k, :], 0.0, *ops))
                diag = ring[:, k, k * P:(k + 1) * P]
                link(v.tensor_tensor(diag, diag, ident[:], ALU.add))
                v.tensor_scalar(to[:, nth(k), k * P:(k + 1) * P], diag, 0.0, *ops).then_inc(mask_done, 1)

            def sub_y_lo(t, c):
                dve.wait_ge(y_hi_done.sem, y_hi_done.level(t, c))
                v.tensor_tensor(y_lo[:, c, :], misc_ps[:, c % MB, 0:PAIR * F], y_hi[:, c, :].bitcast(F32),
                                ALU.subtract).then_inc(y_lo_done.sem, 1)

            def sub_z_lo(t, c):
                dve.wait_ge(z_hi_done.sem, z_hi_done.level(t, c))
                v.tensor_tensor(z_lo[:, c, :], hop_bank(t, c), z_hi[:, c, :].bitcast(F32),
                                ALU.subtract).then_inc(z_lo_done.sem, 1)

            def residual0(t, c):
                if c == 0:
                    dve.wait_ge(x_in.sem, x_in.level(t, 0))
                dve.wait_ge(hop_mm.sem, hop_mm.level(t, K + c))
                v.scalar_tensor_tensor(xn[:, :, c, :], hop_ps[:, c % HB, 0:PAIR * F].rearrange("p (b f) -> p b f", b=PAIR),
                                       0.0, xn[:, :, c, :], ALU.max, ALU.add).then_inc(x1_done.sem, 1)
                dve.wait_ge(x1_done.sem, x1_done.level(t, c))
                for b in range(PAIR):
                    last = v.bn_stats(stats1[:, b, :], xn[:, b, c, :])
                last.then_inc(bn1_done.sem, 1)
                with in_register(dve, bn1_done.level(t, c)) as level:
                    dve.wait_ge(theta_done, 1)
                    dve.wait_ge(bn1_done.sem, level)
                for b in range(PAIR):
                    last = v.bn_aggr(mv1[:, c, b, :], stats1[:, b, :])
                last.then_inc(mv1_done.sem, 1)

            def d_columns(t, b):
                dve.wait_ge(h_ev.sem, h_ev.level(t, (b + 1) * K // 2 - 1))
                v.tensor_copy(d_col[:, b, :], haug[:, b, :, F + 2])
                v.tensor_scalar(d02[:, b, :], haug[:, b, :, F + 2], ALPHA, None, ALU.mult).then_inc(d_ready.sem, 1)

            def masked_max(t, b, k):
                if k == 0:
                    with in_register(dve, d_in[b].level(t, 0)) as level:
                        dve.wait_ge(theta_done, 1)
                        dve.wait_ge(d_in[b].sem, level)
                v.tensor_tensor_reduce(rows_ab[:, b, 1, :].rearrange("p (k q) -> p k q", k=K),
                                       neg[:, k, :].rearrange("p (k q) -> p k q", k=K),
                                       ring[:, D_TILE[b], :].rearrange("p (q k) -> p k q", k=K),
                                       1.0, 4 * MASKED, ALU.add, ALU.max, dmax[:, k:k + 1]).then_inc(max_done.sem, 1)
                with in_register(dve, max_done.level(t, b * K + k)) as level:
                    dve.wait_ge(theta_done, 1)
                    dve.wait_ge(max_done.sem, level)

            def ab_columns(t, b):
                s = haug[:, b, :, F + 1]
                v.tensor_tensor(dmax[:], s, dmax[:], ALU.add).then_inc(logit_done.sem, 1)
                dve.wait_ge(logit_done.sem, logit_done.level(t, b))
                v.scalar_tensor_tensor(dmax[:], dmax[:], ALPHA, dmax[:], ALU.mult, ALU.max).then_inc(m_done.sem, 1)
                dve.wait_ge(m_done.sem, m_done.level(t, b))
                v.tensor_tensor(ab_col[:, b, 0, :], s, dmax[:], ALU.subtract)
                v.scalar_tensor_tensor(ab_col[:, b, 1, :], s, ALPHA, dmax[:], ALU.mult, ALU.subtract).then_inc(ab_ready.sem, 1)

            def exponent(t, s):
                b, k = divmod(s, K)
                if k == 0:
                    dve.wait_ge(a_row_in[b].sem, a_row_in[b].level(t, 0))
                dve.wait_ge(t2_done.sem, t2_done.level(t, s))
                tile = ring[:, s % RING, :].rearrange("p (k q) -> p k q", k=K)
                v.scalar_tensor_tensor(tile, rows_ab[:, b, 0].rearrange("p (q k) -> p k q", k=K),
                                       haug[:, b, k, F + 2:F + 3], tile, ALU.add, ALU.max).then_inc(z_done.sem, 1)

            def mask_p(t, s):
                if not on_pool(s):
                    dve.wait_ge(exp_done[0].sem, exp_done[0].level(t, nth(s)))
                    v.tensor_tensor(ring[:, s % RING, :], ring[:, s % RING, :], mask_t[:, nth(s % K), :],
                                    ALU.min).then_inc(p_done.sem, 1)

            def row_sums(t, b):
                dve.wait_ge(pv_mm.sem, pv_mm.level(t, (b + 1) * K - 1))
                for bank in range(PV_BANKS):
                    lo, hi = bank * PV_PER_BANK, min(K, (bank + 1) * PV_PER_BANK)
                    last = v.reciprocal(rsum[:, b, lo:hi], pv_ps[:, bank, 0:(hi - lo - 1) * PVW + 1:PVW])
                last.then_inc(rsum_done.sem, 1)

            def residual1(t, b, half):
                i, at = 2 * b + half, slice(half * N // 2, (half + 1) * N // 2)
                dve.wait_ge(elu_done.sem, elu_done.level(t, i))
                dve.wait_ge(xres_in[b].sem, xres_in[b].level(t, 0))
                relu, e = rows_ab[:, b, 0, at], rows_ab[:, b, 1, at]
                v.scalar_tensor_tensor(e, e, 1.0, xres[:, b].rearrange("p k f -> p (k f)")[:, at],
                                       ALU.min, ALU.add).then_inc(w_sum.sem, 1)
                dve.wait_ge(w_sum.sem, w_sum.level(t, i))
                v.scalar_tensor_tensor(relu, relu, -1.0, e, ALU.add, ALU.add).then_inc(y_done.sem, 1)

            def moments1(t, b, half):
                i, blocks = 2 * b + half, range(half * K // 2, (half + 1) * K // 2)
                dve.wait_ge(y_done.sem, y_done.level(t, i))
                for k in blocks:
                    last = v.bn_stats(stats2[:, k, :], rows_ab[:, b, 0, k * F:(k + 1) * F])
                last.then_inc(bn2_done.sem, 1)
                with in_register(dve, bn2_done.level(t, i)) as level:
                    dve.wait_ge(theta_done, 1)
                    dve.wait_ge(bn2_done.sem, level)
                for k in blocks:
                    last = v.bn_aggr(mv2[:, b, k, :], stats2[:, k, :])
                last.then_inc(mv2_done.sem, 1)

            def make(u, plan, slot):
                for s in plan["steps"].get(slot, ()):
                    exponent(u, s)
                    newest = s - 1 if s in (K - 1, MADE - 1) else s - plan["ahead"]
                    for m in range(s - plan["ahead"], newest + 1):
                        if m >= 0 and m // K == s // K:
                            mask_p(u, m)

            def one_pass(t, layer0, new, old):
                u, o = t - 1, t - 2
                plan = BESIDE_LAYER0 if layer0 else ALONE
                for c in range(K):
                    if layer0:
                        sub_y_lo(t, c)
                    if old and c == K - 3:
                        exponent(o, 11)
                if not new and layer0:
                    for k in range(K):
                        split_a_lo(k)
                if old:
                    residual1(o, 0, 0)
                    mask_p(o, 10)
                    exponent(o, 12)
                    residual1(o, 0, 1)
                    mask_p(o, 11)
                    exponent(o, 13)
                    mask_p(o, 12)
                if new:
                    d_columns(u, 0)
                if old:
                    exponent(o, 14)
                for slot in range(SLOTS):
                    if layer0 and slot < K:
                        sub_z_lo(t, slot)
                    if layer0 and not new:
                        if slot == 0:
                            constants()
                        (neg_of if slot < K else mask_of)(slot % K)
                    if old:
                        if slot == 0:
                            for half in (0, 1):
                                moments1(o, 0, half)
                            exponent(o, 15)
                        if slot < 2:
                            mask_p(o, 14 + slot)
                        if slot == OLD_SUMS_SLOT:
                            row_sums(o, 1)
                        if slot == plan["old_moments"]:
                            for half in (0, 1):
                                if not new:
                                    residual1(o, 1, half)
                                moments1(o, 1, half)
                    if new:
                        if slot == H1_SLOT + layer0:
                            d_columns(u, 1)
                        if slot in plan["maxes"]:
                            b, blocks = plan["maxes"][slot]
                            for k in blocks:
                                masked_max(u, b, k)
                            if blocks[-1] == K - 1:
                                ab_columns(u, b)
                        if slot == plan["sums"]:
                            row_sums(u, 0)
                    for half in (0, 1):
                        if old and new and slot == plan["old_out"][half]:
                            residual1(o, 1, half)
                    if new:
                        make(u, plan, slot)
                    if layer0 and slot >= K:
                        residual0(t, slot - K)
                    if new and K - 1 in plan["steps"].get(slot, ()):
                        mask_p(u, K - 1)

            passes(dve, one_pass)


def kernel(**inputs):
    import numpy as np
    import concourse.bacc as bacc
    from concourse.bass_utils import run_bass_kernel_spmd

    x, adj = np.asarray(inputs["x"]), np.asarray(inputs["adj"])
    theta, w = np.asarray(inputs["L0_gnn_Theta1"]), np.asarray(inputs["L1_gnn_W"])
    blocks = theta.shape[0] // F
    by_block = lambda a: a.reshape(P, K, P, K).transpose(0, 1, 3, 2).reshape(P, K, N)
    laid = {
        "x": x.reshape(GROUPS, PAIR, P, K, F).transpose(0, 2, 1, 3, 4),
        "xt": x.reshape(GROUPS, PAIR, P, K, F).transpose(0, 4, 3, 1, 2),
        "adj": by_block(adj),
        "adjt": by_block(adj.T),
        "theta": theta.reshape(blocks, F, F).transpose(1, 0, 2),
        "bias": np.asarray(inputs["L0_gnn_bias"]).reshape(1, F),
        "w": w,
        "wt": w.T,
        "a_src": np.asarray(inputs["L1_gnn_a_src"]),
        "a_dst": np.asarray(inputs["L1_gnn_a_dst"]),
        "ident_in": np.eye(P, dtype=np.float32),
    }
    laid = {name: np.ascontiguousarray(a) for name, a in laid.items()}
    nc = bacc.Bacc("TRN2", target_bir_lowering=False, num_devices=1)
    aps = {name: nc.dram_tensor(f"in_{name}", a.shape, mybir.dt.from_np(a.dtype), kind="ExternalInput").ap()
           for name, a in laid.items()}
    out = nc.dram_tensor("out_0", [GROUPS, P, PAIR, K, F], F32, kind="ExternalOutput").ap()
    chebyshev_then_attention(nc, out=out, **aps)
    r = run_bass_kernel_spmd(nc, [{f"in_{name}": a for name, a in laid.items()}], core_ids=[0])
    got = np.asarray(r.results[0]["out_0"])
    return got.reshape(GROUPS, P, PAIR, K, F).transpose(0, 2, 1, 3, 4).reshape(B, N, F)
```
